# Optimizing a Trainium2 kernel written in Bass

```python
import numpy as np
import jax
import jax.numpy as jnp

def _softmax(x, axis=-1):
    return jax.nn.softmax(x, axis=axis)

def _gelu(x):
    return jax.nn.gelu(x, approximate=True)

def _silu(x):
    return jax.nn.silu(x)

def _sigmoid(x):
    return jax.nn.sigmoid(x)

def _layernorm(x, axis=-1, eps=1e-05):
    m = jnp.mean(x, axis=axis, keepdims=True)
    v = jnp.var(x, axis=axis, keepdims=True)
    return (x - m) / jnp.sqrt(v + eps)

def _scatter_add(tgt, idx, src, axis=0):
    return tgt.at[idx].add(src)

def _segment_sum(src, seg, n):
    return jax.ops.segment_sum(src, seg, n)
kernel_name = 'mk_cond_resid_d2_seqx_r2_06663a'

def setup_inputs(seed: int=0):
    np.random.seed(seed)
    _w = jnp.asarray

    def _rec_inputs():
        import jax
        import jax.numpy as jnp
        _rk = jax.random.key(seed)
        x = 7.22e-05 + 1 * jax.random.normal(jax.random.fold_in(_rk, 1), (32, 128, 512), jnp.float32)
        _lenS = 128 - jax.random.randint(jax.random.fold_in(_rk, 7), (32,), 0, max(1, 128 // 4) + 1, jnp.int32)
        _lenS2 = 128 - jax.random.randint(jax.random.fold_in(_rk, 8), (32,), 0, max(1, 128 // 4) + 1, jnp.int32)
        cond_2048 = 0.997298 + 0.498944 * jax.random.normal(jax.random.fold_in(_rk, 11), (32, 1024), jnp.float32)
        return (x, cond_2048)
    x, cond_2048 = _rec_inputs()

    def _L0_cond_setup():
        import jax, jax.numpy as jnp
        import numpy as np
        EPS_IN = 1e-05
        EPS_DM = 1e-08

        def _dcoef(weight, style):
            return jax.lax.rsqrt(jnp.einsum('oi,bi->bo', jnp.square(weight), jnp.square(style)) + EPS_DM)
        key = jax.random.key(seed)
        ks = jax.random.split(key, 7)
        B, S, H = (8, 512, 512)
        lim = 1.0 / np.sqrt(H)
        u = lambda k, shp: jax.random.uniform(k, shp, jnp.float32, -lim, lim)
        return {'x': jax.random.normal(ks[0], (B, S, H), jnp.float32), 'q_weight': u(ks[1], (H, H)), 'k_weight': u(ks[2], (H, H)), 'v_weight': u(ks[3], (H, H)), 'w_weight': u(ks[4], (H, H)), 'u_weight': u(ks[5], (H, H)), 'styles': jax.random.normal(ks[6], (B, 2 * H), jnp.float32) * 0.5 + 1.0, 'num_heads': 16}
    _L0_cond_all = _L0_cond_setup()
    _L0_cond_in = {k: v for k, v in _L0_cond_all.items() if k in ('q_weight', 'k_weight', 'v_weight', 'w_weight', 'u_weight')}
    del _L0_cond_all

    def _L1_cond_setup():
        import jax, jax.numpy as jnp
        import numpy as np
        B, S, D_MODEL, D_INNER, D_STATE = (4, 2048, 512, 1024, 16)
        key = jax.random.key(seed)
        ks = jax.random.split(key, 12)
        inp = {'x': jax.random.normal(ks[0], (B, S, D_MODEL), jnp.float32), 't_emb': jax.random.normal(ks[1], (B, D_INNER), jnp.float32), 'W_in': jax.random.normal(ks[2], (2 * D_INNER, D_MODEL), jnp.float32) * 0.02, 'W_conv': jax.random.normal(ks[3], (D_INNER, 1, 4), jnp.float32) * 0.1, 'b_conv': jnp.zeros((D_INNER,), jnp.float32), 'ln_g': jnp.ones((D_INNER,), jnp.float32), 'ln_b': jnp.zeros((D_INNER,), jnp.float32), 'W_xproj': jax.random.normal(ks[4], (3 * D_STATE, D_INNER), jnp.float32) * 0.02, 'W_dt': jax.random.normal(ks[5], (D_STATE, D_STATE), jnp.float32) * 0.01, 'b_dt': jax.random.uniform(ks[6], (D_STATE,), jnp.float32) * 0.1, 'A_log': jax.random.normal(ks[7], (D_STATE,), jnp.float32) * 0.1, 'D': jnp.ones((D_INNER,), jnp.float32) * 0.1, 'W_out': jax.random.normal(ks[8], (D_MODEL, D_INNER), jnp.float32) * 0.02}
        return inp
    _L1_cond_all = _L1_cond_setup()
    _L1_cond_in = {k: v for k, v in _L1_cond_all.items() if k in ('W_in', 'W_conv', 'b_conv', 'ln_g', 'ln_b', 'W_xproj', 'W_dt', 'b_dt', 'A_log', 'D', 'W_out')}
    del _L1_cond_all
    return {'x': x, 'cond_2048': cond_2048, 'L0_cond_q_weight': _L0_cond_in['q_weight'], 'L0_cond_k_weight': _L0_cond_in['k_weight'], 'L0_cond_v_weight': _L0_cond_in['v_weight'], 'L0_cond_w_weight': _L0_cond_in['w_weight'], 'L0_cond_u_weight': _L0_cond_in['u_weight'], 'L1_cond_W_in': _L1_cond_in['W_in'], 'L1_cond_W_conv': _L1_cond_in['W_conv'], 'L1_cond_b_conv': _L1_cond_in['b_conv'], 'L1_cond_ln_g': _L1_cond_in['ln_g'], 'L1_cond_ln_b': _L1_cond_in['ln_b'], 'L1_cond_W_xproj': _L1_cond_in['W_xproj'], 'L1_cond_W_dt': _L1_cond_in['W_dt'], 'L1_cond_b_dt': _L1_cond_in['b_dt'], 'L1_cond_A_log': _L1_cond_in['A_log'], 'L1_cond_D': _L1_cond_in['D'], 'L1_cond_W_out': _L1_cond_in['W_out']}

def reference(x, cond_2048, L0_cond_q_weight, L0_cond_k_weight, L0_cond_v_weight, L0_cond_w_weight, L0_cond_u_weight, L1_cond_W_in, L1_cond_W_conv, L1_cond_b_conv, L1_cond_ln_g, L1_cond_ln_b, L1_cond_W_xproj, L1_cond_W_dt, L1_cond_b_dt, L1_cond_A_log, L1_cond_D, L1_cond_W_out):
    import jax
    import jax.numpy as jnp

    def _L0_cond_ref(x, q_weight, k_weight, v_weight, w_weight, u_weight, styles, num_heads):
        import jax, jax.numpy as jnp
        import numpy as np
        EPS_IN = 1e-05
        EPS_DM = 1e-08

        def _dcoef(weight, style):
            return jax.lax.rsqrt(jnp.einsum('oi,bi->bo', jnp.square(weight), jnp.square(style)) + EPS_DM)
        B, S, H = x.shape
        nh = num_heads
        d = H // nh
        scale = jnp.asarray(d, x.dtype) ** (-0.5)
        s1 = styles[:, :H]
        s2 = styles[:, H:]
        x = x * s1[:, None, :]
        mu = jnp.mean(x, axis=-1, keepdims=True)
        var = jnp.mean(jnp.square(x - mu), axis=-1, keepdims=True)
        x = (x - mu) * jax.lax.rsqrt(var + EPS_IN)
        q_dc = _dcoef(q_weight, s1)
        k_dc = _dcoef(k_weight, s1)
        v_dc = _dcoef(v_weight, s1)
        w_dc = _dcoef(w_weight, s2)
        u_dc = _dcoef(u_weight, s2)

        def heads(t):
            return t.reshape(B, S, nh, d).transpose(0, 2, 1, 3)
        q = heads(jnp.einsum('bsh,oh->bso', x, q_weight) * q_dc[:, None, :])
        k = heads(jnp.einsum('bsh,oh->bso', x, k_weight) * k_dc[:, None, :])
        v_flat = jnp.einsum('bsh,oh->bso', x, v_weight) * v_dc[:, None, :] * s2[:, None, :]
        skip = v_flat
        v = heads(v_flat)
        attn = jnp.einsum('bhqd,bhkd->bhqk', q, k) * scale
        attn = jax.nn.softmax(attn, axis=-1)
        out = jnp.einsum('bhqk,bhkd->bhqd', attn, v).transpose(0, 2, 1, 3).reshape(B, S, H)
        out = jnp.einsum('bsh,oh->bso', out, w_weight) * w_dc[:, None, :]
        skip = jnp.einsum('bsh,oh->bso', skip, u_weight) * u_dc[:, None, :]
        return out + skip

    def _L1_cond_ref(x, t_emb, W_in, W_conv, b_conv, ln_g, ln_b, W_xproj, W_dt, b_dt, A_log, D, W_out):
        import jax, jax.numpy as jnp
        import numpy as np
        B, S, D_MODEL, D_INNER, D_STATE = (4, 2048, 512, 1024, 16)
        d_inner = W_conv.shape[0]
        d_state = A_log.shape[0]
        xr, gate = jnp.split(x @ W_in.T, 2, axis=-1)
        xr = xr + t_emb[:, None, :]
        xc = jax.lax.conv_general_dilated(xr.transpose(0, 2, 1), W_conv, (1,), [(3, 0)], feature_group_count=d_inner, dimension_numbers=('NCH', 'OIH', 'NCH')) + b_conv[None, :, None]
        xc = jax.nn.silu(xc).transpose(0, 2, 1)
        mu = xc.mean(-1, keepdims=True)
        var = xc.var(-1, keepdims=True)
        xn = (xc - mu) / jnp.sqrt(var + 1e-05) * ln_g + ln_b
        Bm, Cm, dt = jnp.split(xn @ W_xproj.T, 3, axis=-1)
        dt = jnp.tanh(dt @ W_dt.T + b_dt) * 0.01
        A = -jnp.tanh(A_log)
        Ad = 1.0 + dt * A
        Bd = Bm * jnp.minimum(jnp.linalg.norm(xn, axis=-1, keepdims=True), 1.0)
        h0 = jnp.zeros((xn.shape[0], d_state, d_inner), xn.dtype)

        def step(h, inputs):
            ad, bd, xt, ct = inputs
            h = jnp.clip(h * ad[:, :, None] + bd[:, :, None] * xt[:, None, :], -10.0, 10.0)
            yt = jnp.einsum('bd,bdh->bh', ct, h)
            return (h, yt)
        _, ys = jax.lax.scan(step, h0, (Ad.transpose(1, 0, 2), Bd.transpose(1, 0, 2), xn.transpose(1, 0, 2), Cm.transpose(1, 0, 2)))
        y = ys.transpose(1, 0, 2) + D * xn
        return y * jax.nn.silu(gate) @ W_out.T
    x = x + _L0_cond_ref(x, L0_cond_q_weight, L0_cond_k_weight, L0_cond_v_weight, L0_cond_w_weight, L0_cond_u_weight, cond_2048, 16)
    x = x + _L1_cond_ref(x, cond_2048, L1_cond_W_in, L1_cond_W_conv, L1_cond_b_conv, L1_cond_ln_g, L1_cond_ln_b, L1_cond_W_xproj, L1_cond_W_dt, L1_cond_b_dt, L1_cond_A_log, L1_cond_D, L1_cond_W_out)
    return x

_drawn_inputs = setup_inputs


def setup_inputs(seed=0):
    import zlib

    import numpy as np

    out = dict(_drawn_inputs(seed))
    spreads = {'L1_cond_b_conv': (0.0, 0.1),
     'L1_cond_ln_g': (1.0, 0.2),
     'L1_cond_ln_b': (0.0, 0.1),
     'L1_cond_D': (0.10000000149011612, 0.6)}
    factors = {'L1_cond_W_dt': 49.34, 'L1_cond_b_dt': 27.29, 'L1_cond_A_log': 8.0}
    for name, (base, spread) in spreads.items():
        noise = np.random.default_rng([zlib.crc32(name.encode()), seed]).standard_normal(out[name].shape)
        drawn = base * np.exp(spread * noise) if base else spread * noise
        out[name] = jnp.asarray(drawn.astype(out[name].dtype))
    for name, factor in factors.items():
        out[name] = (out[name] * factor).astype(out[name].dtype)
    return out
```

```python
import numpy as np

import concourse.bass as bass
import concourse.mybir as mybir

NB, T, H = 32, 128, 512
HEADS, DH = 16, 32
CI, DS = 1024, 16
P = 128
HM, CM = H // P, CI // P
GB = P // DS
BT = T // GB
EPS_IN, EPS_DM, EPS_LN = 1e-5, 1e-8, 1e-5
LIM = 10.0

INNER, SCAN, OUT = 1, 2 + GB, 2 + 2 * GB
SPANS = [(0, 1), (1, 9), (9, 10), (10, 18), (18, 32), (32, 33), (33, 41), (41, 42), (42, 50)]
SLOTS = BT

ATT_USES = ["xnT", "q", "k", "v", "vT", "s0", "s1", "p0", "s2", "p1", "s3", "p2", "p3", "pv", "w", "u"]
INN_USES = ["xr0", "xr1", "g0", "g1", "c0", "c1", "proj", "projT", "dt"]
OUT_USES = ["yT0", "yT1", "out"]
U0, SUM0, Y0 = 8, 2, 16
QK, VF, WF, UF, TE, NF = 0, HM, 2 * HM, 3 * HM, 4 * HM, 4 * HM + CM

def build(nc, a):
    from contextlib import ExitStack

    f32 = mybir.dt.float32
    ALU = mybir.AluOpType
    ACT = mybir.ActivationFunctionType
    AX = mybir.AxisListType
    ctx = ExitStack()

    def sb(name, shape):
        return ctx.enter_context(nc.sbuf_tensor(name, shape, f32))

    def sem(name):
        return ctx.enter_context(nc.semaphore(name))

    with ctx:
        xn_d = nc.dram_tensor("xn_d", (NB // GB, GB, T, CI), f32, kind="Internal").ap()
        b_d = nc.dram_tensor("b_d", (NB // GB, GB, T, DS), f32, kind="Internal").ap()
        c_d = nc.dram_tensor("c_d", (NB // GB, GB, DS, T), f32, kind="Internal").ap()
        a_d = nc.dram_tensor("a_d", (NB // GB, GB, DS, T), f32, kind="Internal").ap()
        y_d = nc.dram_tensor("y_d", (NB // GB, GB, T, CI), f32, kind="Internal").ap()
        gate_d = nc.dram_tensor("gate_d", (NB, P, CM * T), f32, kind="Internal").ap()
        x1_d = nc.dram_tensor("x1_d", (NB, P, HM * T), f32, kind="Internal").ap()

        w5 = sb("w5", [P, 5, HM, H])
        w_in = sb("w_in", [P, HM, 2 * CI])
        w_out = sb("w_out", [P, CM, H])
        w_x = sb("w_x", [P, CM, 3 * DS])
        w_x0 = sb("w_x0", [P, 3 * DS])
        rows = sb("rows", [P, 3, CI])
        ident = sb("ident", [P, P])
        mask_b = sb("mask_b", [P, BT, GB])
        mask_c = sb("mask_c", [P, 32])
        cvec = sb("cvec", [P, CM, 7])
        table = sb("table", [P, NB, NF])
        small = sb("small", [48, 4])
        w_dt = sb("w_dt", [48, DS])
        a_coef = sb("a_coef", [DS, 1])
        half_n = sb("half_n", [P, 1])
        half_p = sb("half_p", [P, 1])

        prob_t = sb("prob_t", [P, 4, 4, T])
        x_tok = prob_t[:, 0].rearrange("p j t -> p (j t)")
        s1_row = prob_t[:, 1].rearrange("p j t -> p (j t)")
        x_res = prob_t[:, 2]
        fac = sb("fac", [P, 2, NF])
        xn_t = sb("xn_t", [P, HM, T])
        q_t = sb("q_t", [P, HM, T])
        k_bd = sb("k_bd", [P, HM, 4, T])
        v_tok = sb("v_tok", [P, H])
        vs_t = xn_t
        prob = sb("prob", [P, 2, 4, T])
        o_t = q_t
        x1_t = sb("x1_t", [P, HM, T])
        xr = sb("xr", [P, CM, T + 3])
        xc = sb("xc", [P, CM, T])
        th = sb("th", [P, 4, T])
        gate = sb("gate", [P, CM, T])
        xn_tok = sb("xn_tok", [P, CI])
        stat = sb("stat", [P, 2, 6])
        mv = sb("mv", [P, 2])
        rstd = sb("rstd", [P, 2])
        stat2 = sb("stat2", [P, 2, 6])
        mv2 = sb("mv2", [P, 2])
        rstd2 = sb("rstd2", [P, 2])
        nmax = sb("nmax", [P, HEADS])
        rsum = sb("rsum", [P, HEADS])
        rinv = sb("rinv", [P, HEADS])
        norm = sb("norm", [P, 3])
        proj = sb("proj", [P, 3 * DS])
        b_s = sb("b_s", [P, DS])
        proj_t = sb("proj_t", [3 * DS, T])
        dt_t = sb("dt_t", [DS, T])
        a_t = sb("a_t", [DS, T])

        x_blk = sb("x_blk", [P, 2, CI])
        b_blk = sb("b_blk", [P, 2, DS])
        c_blk = sb("c_blk", [P, 2, BT])
        a_blk = sb("a_blk", [P, 2, BT])
        b_bd = sb("b_bd", [P, 2, BT // 2, GB, DS])
        c_bd = sb("c_bd", [P, BT, 32])
        h_new = sb("h_new", [P, CI])
        h = sb("h", [P, 2, CI])
        y_sb = sb("y_sb", [P, 2, 2, H])

        y_tok = sb("y_tok", [P, CI])
        xn_o = sb("xn_o", [P, CI])
        gate_o = sb("gate_o", [P, CM, T])
        x1_o = sb("x1_o", [P, HM, T])

        ones = b_bd[:].rearrange("p f t b d -> p (f t b d)")[:, 0:P]
        cond_t = y_sb[:].rearrange("p f q c -> p (f q c)")[:, 0:2 * HM * NB].rearrange("p (k b) -> p k b", b=NB)

        pu = [ctx.enter_context(nc.psum_tensor(f"pu{i}", [P, CI], f32)) for i in range(2)]
        py = ctx.enter_context(nc.psum_tensor("py", [P, 512], f32))
        pa = ctx.enter_context(nc.psum_tensor("pa", [P, 512], f32))
        pi = ctx.enter_context(nc.psum_tensor("pi", [P, 512], f32))
        po = ctx.enter_context(nc.psum_tensor("po", [P, 512], f32))

        def chunks(ap, n=4):
            return ap.rearrange("p (m t) -> p m t", m=n)

        s_in = sem("inputs_loaded")
        s_zero = sem("constants_set")
        s_sq = sem("squares_ready")
        s_dc = sem("dcoef_sums_in_psum")
        s_dcv = sem("dcoef_sums_kept")
        s_sqrt = sem("sqrt_ready")
        s_a0 = sem("tanh_a_log_ready")
        s_wgb = sem("w_x_scaled")
        s_wsum = sem("column_sums_in_psum")
        s_set = sem("setup_step_done")
        s_table = sem("setup_done")
        att_full, att_free = sem("attention_bank_full"), sem("attention_bank_free")
        inn_full, inn_free = sem("inner_bank_full"), sem("inner_bank_free")
        out_full, out_free = sem("out_bank_full"), sem("out_bank_free")
        s_x = sem("x_loaded")
        s_res = sem("residual_loaded")
        s_fac = sem("factors_ready")
        s_xs = sem("x_styled")
        s_st = sem("stats_ready")
        s_mv = sem("mean_var_ready")
        s_ve = sem("var_eps_ready")
        s_rs = sem("rstd_ready")
        s_xn = sem("xn_ready")
        s_mx = sem("neg_max_ready")
        s_ri = sem("reciprocal_sum_ready")
        s_pr = sem("prob_ready")
        s_xres = sem("x1_with_x_ready")
        s_x1 = sem("x1_ready")
        s_c3 = sem("conv_tap3_ready")
        s_cv = sem("conv_step_done")
        s_th = sem("tanh_xc_ready")
        s_sl = sem("silu_ready")
        s_thg = sem("tanh_gate_ready")
        s_st2 = sem("inner_stats_ready")
        s_mv2 = sem("inner_mean_var_ready")
        s_ve2 = sem("inner_var_eps_ready")
        s_rs2 = sem("inner_rstd_ready")
        s_hat = sem("inner_xhat_ready")
        s_xg = sem("inner_xhat_times_g_ready")
        s_xnt = sem("inner_xn_ready")
        s_ss = sem("sum_of_squares_ready")
        s_ssm = sem("bounded_sum_of_squares_ready")
        s_nm = sem("norm_ready")
        s_b = sem("scaled_b_ready")
        s_a = sem("decay_ready")
        s_x1st = sem("x1_stored")
        s_gst = sem("gate_stored")
        s_xst = sem("xn_stored")
        s_bst = sem("b_stored")
        s_cst = sem("c_stored")
        s_ast = sem("decay_stored")
        s_blk = [sem("block_loaded_even"), sem("block_loaded_odd")]
        s_bbd = sem("b_blockdiag_ready")
        s_cbd = sem("c_blockdiag_ready")
        s_u = sem("update_in_psum")
        s_hn = sem("state_summed")
        s_h = sem("state_clipped")
        s_y = sem("y_in_psum")
        s_yk = sem("y_kept")
        s_yst = [sem("y_stored_even_quarters"), sem("y_stored_odd_quarters")]
        s_ol = sem("out_inputs_loaded")
        s_dx = sem("d_times_xn_ready")
        s_yd = sem("y_plus_d_xn_ready")
        s_fin = sem("result_ready")
        s_out = sem("result_stored")
        s_mark = sem("mark_behind_a_wait")
        BLOCK_DMAS = 2 * GB + 2

        block = ctx.enter_context(nc.Block())


        def iterations(eng, one):
            for first, end in SPANS:
                if end - first == 1:
                    one(first, first % 2, first)
                else:
                    with eng.Fori(0, (end - first) // 2) as pair:
                        for odd in range(2):
                            one(pair * 2 + (first + odd), (first + odd) % 2, first)

        def attends(first):
            return first < NB

        def has_inner(first):
            return INNER <= first < NB + INNER

        def scans(first):
            return SCAN <= first < NB + SCAN

        def outputs(first):
            return OUT <= first < NB + OUT

        def done_of(use, uses, n):
            return n * len(uses) + uses.index(use) + 1

        def before(use, uses, n):
            return n * len(uses) + uses.index(use)

        def row(dram, n):
            return dram[bass.ds(n, 1)].rearrange("o p c -> (o p) c")

        def grouped(dram, n):
            return dram[bass.ds(n // GB, 1), bass.ds(n % GB, 1)].rearrange("g b t c -> (g b t) c")

        def flat(ap):
            return ap.rearrange("p m t -> p (m t)")

        @block.sync
        def _(sp):
            for dst, name in ((w5[:], "w5"), (w_in[:], "w_in"), (w_out[:], "w_out"), (w_x[:], "w_x"),
                              (ident[:], "ident"), (mask_b[:], "mask_b"), (mask_c[:], "mask_c"),
                              (cond_t, "cond_t"), (w_dt[2 * DS:3 * DS, :], "w_dt"),
                              (small[0:DS, 0:1], "b_dt"), (small[0:DS, 1:2], "a_log"), (cvec[:], "cvec")):
                sp.dma_start(dst, a[name]).then_inc(s_in, 16)
            for j, name in enumerate(("ln_g_row", "ln_b_row", "d_row")):
                sp.dma_start(rows[:, j, :], a[name].broadcast_to([P, CI])).then_inc(s_in, 16)

            def load_block(n, par):
                for dst, dram in ((x_blk, xn_d), (b_blk, b_d)):
                    for b in range(GB):
                        sp.dma_start(dst[b * BT:(b + 1) * BT, par, :],
                                     dram[bass.ds(n // GB, 1), b, bass.ds((n % GB) * BT, BT), :]
                                     .rearrange("g t c -> (g t) c")).then_inc(s_blk[par], 16)
                for dst, dram in ((c_blk, c_d), (a_blk, a_d)):
                    sp.dma_start(dst[:, par, :], dram[bass.ds(n // GB, 1), :, :, bass.ds((n % GB) * BT, BT)]
                                 .rearrange("g b d t -> (g b d) t")).then_inc(s_blk[par], 16)

            def store_y(n, quarter):
                sp.wait_ge(s_yk, n * 8 + 2 * quarter + 2)
                for odd in range(2):
                    for half in range(2):
                        q0 = 32 * (2 * odd + half)
                        t0 = (n % GB) * BT + 4 * quarter
                        dst = y_d[bass.ds(n // GB, 1), :, bass.ds(t0, 4), half * H:(half + 1) * H]
                        dst = dst.rearrange("g b (e o) c -> (g b) e o c", o=2)[:, :, odd, :]
                        sp.dma_start(dst, y_sb[q0:q0 + GB, quarter % 2, :, :]).then_inc(s_yst[quarter % 2], 16)

            def one(i, par, first):
                if attends(first):
                    n = i
                    sp.wait_ge(att_free, n * len(ATT_USES))
                    sp.dma_start(x_tok, row(a["x"], n)).then_inc(s_x, 16)
                    sp.dma_start(s1_row, a["cond"][bass.ds(n, 1), 0:H].broadcast_to([P, H])).then_inc(s_x, 16)
                if outputs(first):
                    m = i - OUT
                    for stored in s_yst:
                        sp.wait_ge(stored, (i - SCAN if scans(first) else NB) * 128)
                        sp.sem_inc(s_mark, 1)
                    sp.wait_ge(s_out, m * 16)
                    sp.sem_inc(s_mark, 1)
                    sp.dma_start(y_tok[:], grouped(y_d, m)).then_inc(s_ol, 16)
                    sp.dma_start(xn_o[:], grouped(xn_d, m)).then_inc(s_ol, 16)
                    sp.dma_start(flat(gate_o[:]), row(gate_d, m)).then_inc(s_ol, 16)
                    sp.dma_start(flat(x1_o[:]), row(x1_d, m)).then_inc(s_ol, 16)
                for quarter in range(4):
                    if scans(first):
                        store_y(i - SCAN, quarter)
                    if quarter == 1 and SCAN - 1 <= first < NB + SCAN - 1:
                        n = i - SCAN + 1
                        ready = (i - INNER) if has_inner(first) else NB
                        for stored in (s_xst, s_bst, s_cst, s_ast):
                            sp.wait_ge(stored, ready * 16)
                        sp.sem_inc(s_mark, 1)
                        if first >= SCAN:
                            sp.wait_ge(s_y, Y0 + (i - SCAN) * BT)
                        load_block(n, par ^ 1)
                    if quarter == 1 and has_inner(first):
                        n = i - INNER
                        sp.wait_ge(inn_free, done_of("g1", INN_USES, n))
                        sp.dma_start(row(gate_d, n), flat(gate[:])).then_inc(s_gst, 16)
                    if quarter == 2 and attends(first):
                        sp.wait_ge(att_full, done_of("pv", ATT_USES, i))
                        sp.dma_start(flat(x_res), row(a["x_t"], i)).then_inc(s_res, 16)
                if has_inner(first):
                    n = i - INNER
                    sp.wait_ge(s_xnt, n + 1)
                    sp.dma_start(grouped(xn_d, n), xn_tok[:]).then_inc(s_xst, 16)
                    sp.wait_ge(s_b, n + 1)
                    sp.dma_start(grouped(b_d, n), b_s[:]).then_inc(s_bst, 16)
                    sp.wait_ge(inn_free, done_of("projT", INN_USES, n))
                    sp.dma_start(grouped(c_d, n), proj_t[DS:2 * DS, :]).then_inc(s_cst, 16)
                    sp.wait_ge(s_a, n + 1)
                    sp.dma_start(grouped(a_d, n), a_t[:]).then_inc(s_ast, 16)
                if attends(first):
                    n = i
                    sp.wait_ge(s_x1, n + 1)
                    sp.dma_start(row(x1_d, n), flat(x1_t[:])).then_inc(s_x1st, 16)
                if outputs(first):
                    m = i - OUT
                    sp.wait_ge(s_fin, m + 1)
                    sp.dma_start(row(a["out"], m), flat(x1_o[:])).then_inc(s_out, 16)

            sp.wait_ge(s_table, 1)
            iterations(sp, one)
            sp.wait_ge(s_out, 16 * NB)

        @block.gpsimd
        def _(pool):
            nc.gpsimd.memset(half_n[:], -0.5).then_inc(s_zero, 1)
            nc.gpsimd.memset(half_p[:], 0.5).then_inc(s_zero, 1)
            pool.wait_ge(s_table, 1)

            def scan(s, n, par):
                if s in (0, 8):
                    hh = s // 8
                    if s == 0:
                        pool.wait_ge(s_blk[par], (n + 2 - par) * (8 * BLOCK_DMAS))
                    pool.wait_ge(s_u, U0 + n * BT - 8 + 8 * hh)
                    nc.gpsimd.tensor_tensor(
                        b_bd[:, hh], b_blk[:, par, None, None, :].to_broadcast([P, BT // 2, GB, DS]),
                        mask_b[:, 8 * hh:8 * hh + 8, :, None].to_broadcast([P, BT // 2, GB, DS]),
                        ALU.mult).then_inc(s_bbd, 1)

            def attention(s, n, par):
                if s == 0:
                    pool.wait_ge(s_x, (n + 1) * 32)
                    nc.gpsimd.tensor_tensor(x_tok, x_tok, s1_row, ALU.mult).then_inc(s_xs, 1)
                if s == 1:
                    pool.wait_ge(s_table, 1)
                    pool.wait_ge(s_mv, n + 1)
                    nc.gpsimd.tensor_scalar(rstd[:, 0:1], mv[:, 1:2], EPS_IN, 1.0, ALU.add, ALU.mult).then_inc(s_ve, 1)
                    pool.wait_ge(s_ve, n + 1)
                    nc.gpsimd.tensor_tensor(rstd[:, 1:2], rstd[:, 0:1], half_n[:], ALU.pow).then_inc(s_rs, 1)
                if 6 <= s <= 9:
                    m = s - 6
                    pool.wait_ge(s_ri, n * 4 + m + 1)
                    nc.gpsimd.tensor_tensor(
                        prob[:, m % 2], prob[:, m % 2],
                        rinv[:, 4 * m:4 * m + 4, None].to_broadcast([P, 4, T]), ALU.mult).then_inc(s_pr, 1)
                if s == 12:
                    pool.wait_ge(att_free, done_of("w", ATT_USES, n))
                    pool.wait_ge(s_res, (n + 1) * 16)
                    nc.gpsimd.tensor_tensor(x1_t[:], x1_t[:], x_res, ALU.add).then_inc(s_xres, 1)
                if s == 13:
                    pool.wait_ge(att_free, done_of("u", ATT_USES, n))
                    pool.wait_ge(s_xres, n + 1)
                    nc.gpsimd.tensor_tensor(x1_t[:], x1_t[:], vs_t[:], ALU.add).then_inc(s_x1, 1)

            def inner(s, n, par):
                if s == 9:
                    pool.wait_ge(s_table, 1)
                    pool.wait_ge(s_mv2, n + 1)
                    nc.gpsimd.tensor_scalar(rstd2[:, 0:1], mv2[:, 1:2], 4 * EPS_LN, 1.0, ALU.add, ALU.mult).then_inc(s_ve2, 1)
                    pool.wait_ge(s_ve2, n + 1)
                    nc.gpsimd.tensor_tensor(rstd2[:, 1:2], rstd2[:, 0:1], half_n[:], ALU.pow).then_inc(s_rs2, 1)
                if s == 10:
                    pool.wait_ge(s_hat, n + 1)
                    nc.gpsimd.tensor_tensor(xn_tok[:], xn_tok[:], rows[:, 0, :], ALU.mult).then_inc(s_xg, 1)
                    pool.wait_ge(s_xg, n + 1)
                    nc.gpsimd.tensor_tensor(xn_tok[:], xn_tok[:], rows[:, 1, :], ALU.add).then_inc(s_xnt, 1)
                if s == 13:
                    pool.wait_ge(s_ssm, n + 1)
                    nc.gpsimd.tensor_tensor(norm[:, 2:3], norm[:, 1:2], half_p[:], ALU.pow).then_inc(s_nm, 1)

            def output(s, m, par):
                if s == 2:
                    pool.wait_ge(s_ol, (m + 1) * 64)
                    nc.gpsimd.tensor_tensor(xn_o[:], xn_o[:], rows[:, 2, :], ALU.mult).then_inc(s_dx, 1)
                    pool.wait_ge(s_dx, m + 1)
                    nc.gpsimd.tensor_tensor(y_tok[:], y_tok[:], xn_o[:], ALU.add).then_inc(s_yd, 1)

            def one(i, par, first):
                for s in range(SLOTS):
                    if scans(first):
                        scan(s, i - SCAN, par)
                    if attends(first):
                        attention(s, i, par)
                    if has_inner(first):
                        inner(s, i - INNER, par)
                    if outputs(first):
                        output(s, i - OUT, par)

            iterations(pool, one)

        @block.scalar
        def _(act):
            act.wait_ge(s_in, 16 * 15)
            nc.scalar.activation(flat(th[:])[:, 0:2 * HM * NB], cond_t.rearrange("p k b -> p (k b)"), ACT.Square).then_inc(s_sq, 1)
            for w in range(5):
                if w:
                    act.wait_ge(s_dc, w)
                nc.scalar.activation(k_bd[:].rearrange("p m j t -> p (m j t)"),
                                     w5[:, w].rearrange("p k o -> p (k o)"), ACT.Square).then_inc(s_sq, 1)
            act.wait_ge(s_dcv, 5)
            nc.scalar.activation(xn_tok[:, 0:5 * P], xn_tok[:, 0:5 * P], ACT.Sqrt).then_inc(s_sqrt, 1)
            nc.scalar.activation(a_coef[:], small[0:DS, 1:2], ACT.Tanh).then_inc(s_a0, 1)
            act.wait_ge(s_table, 1)

            def scan(s, n, par):
                if s % 2 == 1:
                    p = s // 2
                    act.wait_ge(s_y, Y0 + n * BT + s + 1)
                    if p % 2 == 0:
                        act.wait_ge(s_yst[(p // 2) % 2], n * 128 + (p // 4) * 64)
                    nc.scalar.activation(y_sb[:, (p // 2) % 2, p % 2, :], py[:], ACT.Copy).then_inc(s_yk, 1)

            def attention(s, n, par):
                def drain(use, dst, src):
                    act.wait_ge(att_full, done_of(use, ATT_USES, n))
                    nc.scalar.activation(dst, src, ACT.Copy).then_inc(att_free, 1)

                def exponentials(m):
                    act.wait_ge(s_mx, n * 4 + m + 1)
                    if m >= 2:
                        act.wait_ge(att_full, done_of(f"p{m - 2}", ATT_USES, n))
                    for j in range(4):
                        hd = 4 * m + j
                        last = nc.scalar.activation(prob[:, m % 2, j, :], chunks(pa[:])[:, j, :], ACT.Exp,
                                                    bias=nmax[:, hd:hd + 1], accum_out=rsum[:, hd:hd + 1])
                    last.then_inc(att_free, 1)

                if s == 2:
                    act.wait_ge(s_x1, n)
                    drain("xnT", xn_t[:], chunks(pa[:]))
                if s == 3:
                    act.wait_ge(att_full, done_of("k", ATT_USES, n))
                    for j in range(4):
                        r = slice(32 * j, 32 * j + 32)
                        last = nc.scalar.activation(k_bd[r, :, j, :], chunks(pa[r, :]), ACT.Copy)
                    last.then_inc(att_free, 1)
                if s == 4:
                    drain("v", v_tok[:], pa[:])
                if s in (8, 10):
                    drain(f"p{s - 7}", prob_t[:, s - 7], chunks(pa[:]))
                if 5 <= s <= 8:
                    exponentials(s - 5)

            def inner(s, n, par):
                if s in (0, 1):
                    act.wait_ge(inn_free, done_of(f"xr{s}", INN_USES, n))
                    for c in range(4 * s, 4 * s + 4):
                        last = nc.scalar.activation(xc[:, c, :], xr[:, c, 3:3 + T], ACT.Identity,
                                                    bias=cvec[:, c, 4:5], scale=cvec[:, c, 3:4])
                    last.then_inc(s_c3, 1)
                if s in (2, 3):
                    hh = s - 2
                    act.wait_ge(inn_full, done_of(f"g{hh}", INN_USES, n))
                    act.wait_ge(s_sl, n * 2)
                    nc.scalar.activation(th[:], chunks(pi[:]), ACT.Tanh, scale=0.5).then_inc(s_thg, 1)
                if s in (4, 5):
                    hh = s - 4
                    act.wait_ge(s_cv, n * 24 + 12 * hh + 12)
                    act.wait_ge(inn_free, done_of("g1", INN_USES, n))
                    act.wait_ge(s_sl, n * 2 + hh)
                    nc.scalar.activation(th[:], xc[:, 4 * hh:4 * hh + 4], ACT.Tanh, scale=0.5).then_inc(s_th, 1)
                if s in (6, 7):
                    hh = s - 6
                    act.wait_ge(inn_full, done_of(f"c{hh}", INN_USES, n))
                    if hh == 0:
                        act.wait_ge(s_xst, n * 16)
                    nc.scalar.activation(xn_tok[:, H * hh:H * hh + H], pi[:], ACT.Copy).then_inc(inn_free, 1)
                if s == 12:
                    act.wait_ge(s_xnt, n + 1)
                    act.wait_ge(inn_full, done_of("proj", INN_USES, n))
                    nc.scalar.activation(flat(xc[:]), xn_tok[:], ACT.Square, accum_out=norm[:, 0:1]).then_inc(s_ss, 1)
                if s == 13:
                    act.wait_ge(inn_full, done_of("projT", INN_USES, n))
                    act.wait_ge(s_cst, n * 16)
                    nc.scalar.activation(proj_t[:], pi[0:3 * DS, 0:T], ACT.Copy).then_inc(inn_free, 1)
                if s == 14:
                    act.wait_ge(inn_full, done_of("dt", INN_USES, n))
                    nc.scalar.activation(dt_t[:], pi[0:DS, 0:T], ACT.Tanh, bias=small[0:DS, 0:1]).then_inc(inn_free, 1)

            def one(i, par, first):
                for s in range(SLOTS):
                    if scans(first) and s:
                        scan(s - 1, i - SCAN, par)
                    if attends(first):
                        attention(s, i, par)
                    if has_inner(first):
                        inner(s, i - INNER, par)
                if scans(first):
                    scan(SLOTS - 1, i - SCAN, par)

            iterations(act, one)

        @block.vector
        def _(dve):
            count = [0]

            def step(ins):
                count[0] += 1
                ins.then_inc(s_set, 1)
                dve.wait_ge(s_set, count[0])

            nc.vector.memset(ones, 1.0).then_inc(s_u, U0)
            nc.vector.memset(xr[:, :, 0:3], 0.0).then_inc(s_hn, SUM0)
            nc.vector.memset(a_t[:, 0:1], 0.0).then_inc(s_y, Y0)
            nc.vector.memset(h[:], 0.0)
            dve.wait_ge(s_in, 16 * 15)
            wg, wb = flat(gate[:])[:, 0:CM * 48], flat(xc[:])[:, 0:CM * 48]
            for dst, col in ((wg, 5), (wb, 6)):
                step(nc.vector.tensor_tensor(chunks(dst, CM), w_x[:], cvec[:, :, col:col + 1].to_broadcast([P, CM, 48]), ALU.mult))
            step(nc.vector.memset(mv[:], 0.0))
            nc.vector.memset(mv2[:], 0.0).then_inc(s_wgb, 1)
            dve.wait_ge(s_wsum, 1)
            step(nc.vector.tensor_scalar(proj[:], pi[:, 0:48], 1.0 / CI, None, ALU.mult))
            step(nc.vector.tensor_tensor(w_x[:], chunks(wg, CM), proj[:, None, :].to_broadcast([P, CM, 48]), ALU.subtract))
            step(nc.vector.tensor_copy(w_x0[:], pi[:, 48:96]))
            for w in range(5):
                dve.wait_ge(s_dc, w + 1)
                nc.vector.tensor_scalar(xn_tok[:, w * P:(w + 1) * P], pa[:, 0:P], EPS_DM, None, ALU.add).then_inc(s_dcv, 1)
            dve.wait_ge(s_sqrt, 1)
            dve.wait_ge(s_dcv, 5)
            step(nc.vector.reciprocal(xn_tok[:, 0:5 * P], xn_tok[:, 0:5 * P]))
            dc = xn_tok[:, 0:5 * P].rearrange("p (w m b) -> p w m b", w=5, m=HM)

            def column(c, n):
                return table[:, :, c:c + n].rearrange("p b m -> p m b")

            step(nc.vector.scalar_tensor_tensor(out=column(QK, HM), in0=dc[:, 0], scalar=DH ** -0.5, in1=dc[:, 1],
                                                op0=ALU.mult, op1=ALU.mult))
            step(nc.vector.tensor_tensor(column(VF, HM), dc[:, 2], cond_t[:, HM:2 * HM, :], ALU.mult))
            step(nc.vector.tensor_copy(column(WF, HM), dc[:, 3]))
            step(nc.vector.tensor_copy(column(UF, HM), dc[:, 4]))
            step(nc.vector.tensor_copy(column(TE, CM), cond_t))
            dve.wait_ge(s_a0, 1)
            step(nc.vector.tensor_scalar(a_coef[:], a_coef[:], -0.01, None, ALU.mult))
            dve.wait_ge(s_zero, 2)
            step(nc.vector.memset(k_bd[:].rearrange("p m j t -> p (m j t)"), 0.0))
            nc.vector.memset(x1_o[:], 0.0).then_inc(s_table, 1)

            def scan(s, n, par):
                if s == 0:
                    dve.wait_ge(s_blk[par], (n + 2 - par) * (8 * BLOCK_DMAS))
                    dve.wait_ge(s_y, Y0 + n * BT)
                    nc.vector.tensor_tensor(c_bd[:], c_blk[:, par, :, None].to_broadcast([P, BT, 32]),
                                            mask_c[:, None, :].to_broadcast([P, BT, 32]), ALU.mult).then_inc(s_cbd, 1)
                t = n * BT + s
                dve.wait_ge(s_u, U0 + t + 1)
                dve.wait_ge(s_h, t)
                nc.vector.scalar_tensor_tensor(out=h_new[:], in0=h[:, (s + 1) % 2, :], scalar=a_blk[:, par, s:s + 1],
                                               in1=pu[s % 2][:], op0=ALU.mult, op1=ALU.add).then_inc(s_hn, 1)
                dve.wait_ge(s_hn, SUM0 + t + 1)
                dve.wait_ge(s_y, Y0 + t - 1)
                nc.vector.tensor_scalar(h[:, s % 2, :], h_new[:], -LIM, LIM, ALU.max, ALU.min).then_inc(s_h, 1)

            def attention(s, n, par):
                def factors(c):
                    return fac[:, par, c:c + HM, None].to_broadcast([P, HM, T])

                def scaled(use, dst, c):
                    dve.wait_ge(att_full, done_of(use, ATT_USES, n))
                    nc.vector.tensor_tensor(dst, chunks(pa[:]), factors(c), ALU.mult).then_inc(att_free, 1)

                if s == 0:
                    nc.vector.tensor_copy(fac[:, par, :], table[:, bass.ds(n, 1), :].rearrange("p o c -> p (o c)")).then_inc(s_fac, 1)
                    dve.wait_ge(s_xs, n + 1)
                    nc.vector.bn_stats(stat[:, 0, :], x_tok).then_inc(s_st, 1)
                    dve.wait_ge(s_table, 1)
                    dve.wait_ge(s_st, n + 1)
                    nc.vector.bn_aggr(mv[:], stat[:, 0, :]).then_inc(s_mv, 1)
                if s == 2:
                    dve.wait_ge(s_rs, n + 1)
                    nc.vector.tensor_scalar(x_tok, x_tok, mv[:, 0:1], rstd[:, 1:2], ALU.subtract, ALU.mult).then_inc(s_xn, 1)
                if s == 3:
                    dve.wait_ge(s_fac, n + 1)
                    scaled("q", q_t[:], QK)
                if s == 4:
                    scaled("vT", vs_t[:], VF)
                if 6 <= s <= 9:
                    m = s - 6
                    dve.wait_ge(att_free, done_of(f"s{m}", ATT_USES, n))
                    nc.vector.reciprocal(rinv[:, 4 * m:4 * m + 4], rsum[:, 4 * m:4 * m + 4]).then_inc(s_ri, 1)
                if s in (7, 9):
                    m = s - 7
                    dve.wait_ge(att_full, done_of(f"p{m}", ATT_USES, n))
                    nc.vector.tensor_copy(prob_t[:, m], chunks(pa[:])).then_inc(att_free, 1)
                if 5 <= s <= 8:
                    m = s - 5
                    dve.wait_ge(att_full, done_of(f"s{m}", ATT_USES, n))
                    nc.vector.tensor_reduce(nmax[:, 4 * m:4 * m + 4], chunks(pa[:]), AX.X, ALU.max, negate=True).then_inc(s_mx, 1)
                if s == 11:
                    scaled("pv", o_t[:], VF)
                if s == 12:
                    dve.wait_ge(s_x1st, n * 16)
                    scaled("w", x1_t[:], WF)
                if s == 13:
                    scaled("u", vs_t[:], UF)

            def inner(s, n, par):
                if s in (0, 1):
                    dve.wait_ge(inn_full, done_of(f"xr{s}", INN_USES, n))
                    te = fac[:, par ^ 1, TE + 4 * s:TE + 4 * s + 4, None].to_broadcast([P, 4, T])
                    nc.vector.tensor_tensor(xr[:, 4 * s:4 * s + 4, 3:], chunks(pi[:]), te, ALU.add).then_inc(inn_free, 1)
                if s in (1, 2):
                    hh = s - 1
                    dve.wait_ge(s_c3, n * 2 + hh + 1)
                    for k in range(3):
                        for c in range(4 * hh, 4 * hh + 4):
                            if k:
                                dve.wait_ge(s_cv, n * 24 + 12 * hh + 4 * (k - 1) + c % 4 + 1)
                            nc.vector.scalar_tensor_tensor(out=xc[:, c, :], in0=xr[:, c, k:k + T], scalar=cvec[:, c, k:k + 1],
                                                           in1=xc[:, c, :], op0=ALU.mult, op1=ALU.add).then_inc(s_cv, 1)
                if s in (2, 3):
                    hh = s - 2
                    dve.wait_ge(s_thg, n * 2 + hh + 1)
                    if hh == 0:
                        dve.wait_ge(s_gst, n * 16)
                    nc.vector.scalar_tensor_tensor(out=gate[:, 4 * hh:4 * hh + 4], in0=th[:], scalar=1.0,
                                                   in1=chunks(pi[:]), op0=ALU.add, op1=ALU.mult).then_inc(inn_free, 1)
                if s in (4, 5):
                    hh = s - 4
                    dve.wait_ge(s_th, n * 2 + hh + 1)
                    nc.vector.scalar_tensor_tensor(out=xc[:, 4 * hh:4 * hh + 4], in0=th[:], scalar=1.0,
                                                   in1=xc[:, 4 * hh:4 * hh + 4], op0=ALU.add, op1=ALU.mult).then_inc(s_sl, 1)
                if s in (7, 8):
                    hh = s - 7
                    dve.wait_ge(inn_free, done_of(f"c{hh}", INN_USES, n))
                    nc.vector.bn_stats(stat2[:, hh, :], xn_tok[:, H * hh:H * hh + H]).then_inc(s_st2, 1)
                if s == 8:
                    dve.wait_ge(s_table, 1)
                    dve.wait_ge(s_st2, n * 2 + 2)
                    nc.vector.bn_aggr(mv2[:], stat2[:]).then_inc(s_mv2, 1)
                if s == 10:
                    dve.wait_ge(s_rs2, n + 1)
                    nc.vector.tensor_scalar(xn_tok[:], xn_tok[:], mv2[:, 0:1], rstd2[:, 1:2], ALU.subtract, ALU.mult).then_inc(s_hat, 1)
                    dve.wait_ge(inn_full, done_of("proj", INN_USES, n))
                    nc.vector.scalar_tensor_tensor(out=proj[:], in0=pi[:, 0:48], scalar=rstd2[:, 1:2], in1=w_x0[:],
                                                   op0=ALU.mult, op1=ALU.add).then_inc(inn_free, 1)
                if s == 13:
                    dve.wait_ge(s_ss, n + 1)
                    nc.vector.tensor_scalar(norm[:, 1:2], norm[:, 0:1], 1.0, None, ALU.min).then_inc(s_ssm, 1)
                if s == 15:
                    dve.wait_ge(inn_free, done_of("dt", INN_USES, n))
                    dve.wait_ge(s_nm, n + 1)
                    dve.wait_ge(s_bst, n * 16)
                    nc.vector.tensor_scalar(b_s[:], proj[:, 0:DS], norm[:, 2:3], None, ALU.mult).then_inc(s_b, 1)
                    dve.wait_ge(s_ast, n * 16)
                    nc.vector.tensor_scalar(a_t[:, 1:T], dt_t[:, 1:T], a_coef[:], 1.0, ALU.mult, ALU.add).then_inc(s_a, 1)

            def output(s, m, par):
                if s in (4, 6):
                    hh = (s - 4) // 2
                    dve.wait_ge(out_full, done_of(f"yT{hh}", OUT_USES, m))
                    g = gate_o[:, 4 * hh:4 * hh + 4]
                    nc.vector.tensor_tensor(g, g, chunks(po[:]), ALU.mult).then_inc(out_free, 1)
                if s == 11:
                    dve.wait_ge(out_full, done_of("out", OUT_USES, m))
                    nc.vector.scalar_tensor_tensor(out=x1_o[:], in0=chunks(po[:]), scalar=0.5, in1=x1_o[:],
                                                   op0=ALU.mult, op1=ALU.add).then_inc(s_fin, 1)

            def one(i, par, first):
                for s in range(SLOTS):
                    if scans(first):
                        scan(s, i - SCAN, par)
                    if attends(first):
                        attention(s, i, par)
                    if has_inner(first):
                        inner(s, i - INNER, par)
                    if outputs(first):
                        output(s, i - OUT, par)

            iterations(dve, one)

        @block.tensor
        def _(pe):
            pe.wait_ge(s_wgb, 1)
            pe.wait_ge(s_set, 3)
            for j, src in enumerate((flat(gate[:]), flat(xc[:]))):
                for k in range(CM):
                    last = nc.tensor.matmul(pi[:, 48 * j:48 * j + 48], ones, src[:, 48 * k:48 * k + 48],
                                            start=(k == 0), stop=(k == CM - 1))
            last.then_inc(s_wsum, 1)
            squares = k_bd[:].rearrange("p m j t -> p m (j t)")
            for w in range(5):
                pe.wait_ge(s_sq, w + 2)
                if w:
                    pe.wait_ge(s_dcv, w)
                style = HM * (w > 2)
                for m in range(HM):
                    for k in range(HM):
                        last = nc.tensor.matmul(pa[:, NB * m:NB * m + NB], squares[:, k, P * m:P * m + P],
                                                flat(th[:])[:, NB * (style + k):NB * (style + k + 1)],
                                                start=(k == 0), stop=(k == HM - 1))
                last.then_inc(s_dc, 1)
            pe.wait_ge(s_table, 1)

            def product(dst, w, rhs, m):
                for k in range(len(rhs)):
                    last = nc.tensor.matmul(dst, w[:, k, P * m:P * m + P], rhs[k],
                                            start=(k == 0), stop=(k == len(rhs) - 1))
                return last

            def update(s, n, par):
                hh = s // 8
                if s == 0:
                    pe.wait_ge(s_blk[par], (n + 2 - par) * (8 * BLOCK_DMAS))
                if s % 8 == 0:
                    pe.wait_ge(s_bbd, n * 2 + hh + 1)
                pe.wait_ge(s_hn, SUM0 + n * BT + s - 1)
                lhs = b_bd[:, hh, s % 8].rearrange("p b d -> p (b d)")
                for half in range(2):
                    r = slice(H * half, H * half + H)
                    last = nc.tensor.matmul(pu[s % 2][:, r], lhs, x_blk[:, par, r], start=True, stop=True)
                last.then_inc(s_u, 1)

            def read_out(s, n, par):
                if s == 0:
                    pe.wait_ge(s_cbd, n + 1)
                if s % 2 == 0:
                    pe.wait_ge(s_yk, n * 8 + s // 2)
                pe.wait_ge(s_h, n * BT + s + 1)
                for half in range(2):
                    q0 = 32 * (2 * (s % 2) + half)
                    last = nc.tensor.matmul(py[q0:q0 + 32, :], c_bd[:, s, :], h[:, s % 2, H * half:H * half + H],
                                            start=True, stop=True)
                last.then_inc(s_y, 1)

            def attention(s, n, par):
                def begin(use):
                    pe.wait_ge(att_free, before(use, ATT_USES, n))

                def transposes(use, src):
                    begin(use)
                    for j in range(4):
                        last = nc.tensor.transpose(pa[:, P * j:P * j + P], src(j), ident[:])
                    last.then_inc(att_full, 1)

                def layer(use, w, src):
                    begin(use)
                    for m in range(HM):
                        last = product(pa[:, P * m:P * m + P], w5[:, w], [src[:, k, :] for k in range(HM)], m)
                    last.then_inc(att_full, 1)

                def scores(m):
                    begin(f"s{m}")
                    nc.tensor.matmul(pa[:], q_t[:, m, :], k_bd[:, m].rearrange("p j t -> p (j t)"),
                                     start=True, stop=True).then_inc(att_full, 1)

                def turned(m):
                    pe.wait_ge(s_pr, n * 4 + m + 1)
                    transposes(f"p{m}", lambda j: prob[:, m % 2, j, :])

                if s == 2:
                    pe.wait_ge(s_xn, n + 1)
                    transposes("xnT", lambda j: x_tok[:, P * j:P * j + P])
                if s == 3:
                    layer("q", 0, xn_t)
                    layer("k", 1, xn_t)
                if s == 4:
                    begin("v")
                    for k in range(HM):
                        last = nc.tensor.matmul(pa[:], xn_t[:, k, :], w5[:, 2, k, :], start=(k == 0), stop=(k == HM - 1))
                    last.then_inc(att_full, 1)
                    transposes("vT", lambda j: v_tok[:, P * j:P * j + P])
                if s == 5:
                    scores(0)
                if s == 6:
                    scores(1)
                if s == 7:
                    turned(0)
                    scores(2)
                if s == 8:
                    turned(1)
                    scores(3)
                if s == 9:
                    turned(2)
                if s == 10:
                    turned(3)
                if s == 11:
                    begin("pv")
                    for m in range(HM):
                        for j in range(4):
                            hd = 4 * m + j
                            last = nc.tensor.matmul(pa[32 * j:32 * j + 32, P * m:P * m + P], v_tok[:, DH * hd:DH * hd + DH],
                                                    prob_t[:, m, j, :], start=True, stop=True)
                    last.then_inc(att_full, 1)
                if s == 12:
                    layer("w", 3, o_t)
                if s == 13:
                    layer("u", 4, vs_t)

            def inner(s, n, par):
                def begin(use):
                    pe.wait_ge(inn_free, before(use, INN_USES, n))

                if s < 4:
                    use = ("xr0", "xr1", "g0", "g1")[s]
                    if s == 0:
                        pe.wait_ge(s_x1, n + 1)
                    begin(use)
                    for m in range(4):
                        last = product(pi[:, P * m:P * m + P], w_in, [x1_t[:, k, :] for k in range(HM)], 4 * s + m)
                    last.then_inc(inn_full, 1)
                if s in (6, 7):
                    hh = s - 6
                    pe.wait_ge(s_sl, n * 2 + hh + 1)
                    begin(f"c{hh}")
                    for j in range(4):
                        last = nc.tensor.transpose(pi[:, P * j:P * j + P], xc[:, 4 * hh + j, :], ident[:])
                    last.then_inc(inn_full, 1)
                if s == 8:
                    begin("proj")
                    for k in range(CM):
                        last = nc.tensor.matmul(pi[:, 0:48], xc[:, k, :], w_x[:, k, :], start=(k == 0), stop=(k == CM - 1))
                    last.then_inc(inn_full, 1)
                if s == 12:
                    begin("projT")
                    pe.sem_inc(s_mark, 1)
                    nc.tensor.transpose(pi[0:48, 0:T], proj[:], ident[:]).then_inc(inn_full, 1)
                if s == 14:
                    begin("dt")
                    pe.sem_inc(s_mark, 1)
                    nc.tensor.matmul(pi[0:DS, 0:T], w_dt[2 * DS:3 * DS, :], proj_t[2 * DS:3 * DS, :],
                                     start=True, stop=True).then_inc(inn_full, 1)

            def output(s, m, par):
                if s in (4, 6):
                    hh = (s - 4) // 2
                    pe.wait_ge(s_yd, m + 1)
                    pe.wait_ge(out_free, m * 2 + hh)
                    if hh == 0:
                        pe.wait_ge(s_fin, m)
                    for j in range(4):
                        c0 = P * (4 * hh + j)
                        last = nc.tensor.transpose(po[:, P * j:P * j + P], y_tok[:, c0:c0 + P], ident[:])
                    last.then_inc(out_full, 1)
                if 7 <= s <= 10:
                    if s == 7:
                        pe.wait_ge(out_free, m * 2 + 2)
                    last = product(po[:, P * (s - 7):P * (s - 6)], w_out, [gate_o[:, k, :] for k in range(CM)], s - 7)
                    if s == 10:
                        last.then_inc(out_full, 1)

            def one(i, par, first):
                for s in range(SLOTS):
                    if scans(first):
                        update(s, i - SCAN, par)
                        if s:
                            read_out(s - 1, i - SCAN, par)
                    if attends(first):
                        attention(s, i, par)
                    if has_inner(first):
                        inner(s, i - INNER, par)
                    if outputs(first):
                        output(s, i - OUT, par)
                if scans(first):
                    read_out(SLOTS - 1, i - SCAN, par)

            iterations(pe, one)


def kernel(x, cond_2048, L0_cond_q_weight, L0_cond_k_weight, L0_cond_v_weight, L0_cond_w_weight, L0_cond_u_weight,
           L1_cond_W_in, L1_cond_W_conv, L1_cond_b_conv, L1_cond_ln_g, L1_cond_ln_b, L1_cond_W_xproj, L1_cond_W_dt,
           L1_cond_b_dt, L1_cond_A_log, L1_cond_D, L1_cond_W_out):
    import concourse.bacc as bacc
    from concourse.bass_utils import run_bass_kernel_spmd

    def turned(w):
        w = np.asarray(w)
        o, i = w.shape
        return w.T.reshape(i // P, P, o).transpose(1, 0, 2)

    def by_channel(v):
        v = np.asarray(v)
        return v.reshape(CM, P, -1).transpose(1, 0, 2)

    x, cond = np.asarray(x), np.asarray(cond_2048)
    row, step = np.arange(P)[:, None], np.arange(BT)[None, :]
    arrays = {
        "x": x,
        "x_t": x.transpose(0, 2, 1).reshape(NB, HM, P, T).transpose(0, 2, 1, 3).reshape(NB, P, HM * T),
        "cond": cond,
        "cond_t": cond.T.reshape(2 * HM, P, NB).transpose(1, 0, 2),
        "w5": np.stack([turned(w) for w in (L0_cond_q_weight, L0_cond_k_weight, L0_cond_v_weight,
                                            L0_cond_w_weight, L0_cond_u_weight)], 1),
        "w_in": turned(L1_cond_W_in),
        "w_out": turned(L1_cond_W_out),
        "w_x": turned(L1_cond_W_xproj),
        "w_dt": np.asarray(L1_cond_W_dt).T,
        "b_dt": np.asarray(L1_cond_b_dt)[:, None],
        "a_log": np.asarray(L1_cond_A_log)[:, None],
        "cvec": np.concatenate([by_channel(np.asarray(L1_cond_W_conv).reshape(CI, 4)), by_channel(L1_cond_b_conv),
                                by_channel(L1_cond_ln_g), by_channel(L1_cond_ln_b)], 2),
        "ln_g_row": np.asarray(L1_cond_ln_g)[None, :],
        "ln_b_row": np.asarray(L1_cond_ln_b)[None, :],
        "d_row": np.asarray(L1_cond_D)[None, :],
        "ident": np.eye(P, dtype=np.float32),
        "mask_b": ((row % BT == step)[:, :, None] & (row // BT == np.arange(GB)[None, :])[:, None, :]).astype(np.float32),
        "mask_c": (row // DS == np.arange(32)[None, :]).astype(np.float32),
    }
    arrays = {k: np.ascontiguousarray(v) for k, v in arrays.items()}
    nc = bacc.Bacc("TRN2", target_bir_lowering=False, num_devices=1)
    aps = {k: nc.dram_tensor(f"in_{k}", v.shape, mybir.dt.from_np(v.dtype), kind="ExternalInput").ap()
           for k, v in arrays.items()}
    aps["out"] = nc.dram_tensor("out_t", (NB, P, HM * T), mybir.dt.float32, kind="ExternalOutput").ap()
    build(nc, aps)
    r = run_bass_kernel_spmd(nc, [{f"in_{k}": v for k, v in arrays.items()}], core_ids=[0])
    out = np.asarray(r.results[0]["out_t"])
    return out.reshape(NB, P, HM, T).transpose(0, 3, 2, 1).reshape(NB, T, H)
```

```python
import numpy as np

import concourse.bass as bass
import concourse.mybir as mybir

NB, T, H = 32, 128, 512
HEADS, DH = 16, 32
CI, DS = 1024, 16
P = 128
HM, CM = H // P, CI // P
GB = P // DS
BT = T // GB
TERMS = 4
QT = P // (TERMS * GB)
QUARTERS = BT // QT
EPS_IN, EPS_DM, EPS_LN = 1e-5, 1e-8, 1e-5
LIM = 10.0

INNER, SCAN, OUT = 1, 2 + GB, 2 + 2 * GB
SPANS = [(0, 1), (1, 9), (9, 10), (10, 18), (18, 32), (32, 33), (33, 41), (41, 42), (42, 50)]
SLOTS = BT

ATT_USES = ["xnT", "q", "k", "v", "vT", "s0", "s1", "p0", "s2", "p1", "s3", "p2", "p3", "pv", "w", "u"]
INN_USES = ["xr0", "xr1", "g0", "g1", "c0", "c1", "proj", "projT", "dt"]
OUT_USES = ["yT0", "yT1", "out"]
U0, SUM0, Y0, START = 5, 2, 16, 1
QK, VF, WF, UF, TE, NF = 0, HM, 2 * HM, 3 * HM, 4 * HM, 4 * HM + CM

def build(nc, a):
    from contextlib import ExitStack

    f32, f32r = mybir.dt.float32, mybir.dt.float32r
    ALU = mybir.AluOpType
    ACT = mybir.ActivationFunctionType
    AX = mybir.AxisListType
    ctx = ExitStack()

    def sb(name, shape, dtype=f32):
        return ctx.enter_context(nc.sbuf_tensor(name, shape, dtype))

    def sem(name):
        return ctx.enter_context(nc.semaphore(name))

    with ctx:
        xn_d = nc.dram_tensor("xn_d", (NB // GB, T // QT, GB, QT, CI), f32, kind="Internal").ap()
        b_d = nc.dram_tensor("b_d", (NB // GB, T // QT, GB, QT, DS), f32, kind="Internal").ap()
        c_d = nc.dram_tensor("c_d", (NB // GB, GB, DS, T), f32, kind="Internal").ap()
        a_d = nc.dram_tensor("a_d", (NB // GB, GB, DS, T), f32, kind="Internal").ap()
        y_d = nc.dram_tensor("y_d", (NB // GB, GB, T, CI), f32, kind="Internal").ap()
        gate_d = nc.dram_tensor("gate_d", (NB, P, CM * T), f32, kind="Internal").ap()
        x1_d = nc.dram_tensor("x1_d", (NB, P, HM * T), f32, kind="Internal").ap()

        w5 = sb("w5", [P, 5, HM, H])
        w_in = sb("w_in", [P, HM, 2 * CI])
        w_out = sb("w_out", [P, CM, H])
        w_x = sb("w_x", [P, CM, 3 * DS])
        w_x0 = sb("w_x0", [P, 3 * DS])
        rows = sb("rows", [P, 3, CI])
        ident = sb("ident", [P, P])
        mask_b = sb("mask_b", [P, QT, GB])
        mask_c = sb("mask_c", [P, 32])
        cvec = sb("cvec", [P, CM, 7])
        table = sb("table", [P, NB, NF])
        small = sb("small", [48, 4])
        w_dt = sb("w_dt", [48, DS])
        a_coef = sb("a_coef", [DS, 1])
        half_n = sb("half_n", [P, 1])
        half_p = sb("half_p", [P, 1])

        prob_t = sb("prob_t", [P, 4, 4, T])
        x_tok = prob_t[:, 0].rearrange("p j t -> p (j t)")
        s1_row = prob_t[:, 1].rearrange("p j t -> p (j t)")
        x_res = prob_t[:, 2]
        fac = sb("fac", [P, 2, NF])
        xn_t = sb("xn_t", [P, HM, T])
        q_t = sb("q_t", [P, HM, T])
        k_bd = sb("k_bd", [P, HM, 4, T])
        v_tok = sb("v_tok", [P, H])
        vs_t = xn_t
        prob = sb("prob", [P, 2, 4, T])
        o_t = q_t
        x1_t = sb("x1_t", [P, HM, T])
        xr = sb("xr", [P, CM, T + 3])
        xc = sb("xc", [P, CM, T])
        th = sb("th", [P, 4, T])
        gate = sb("gate", [P, CM, T])
        xn_tok = sb("xn_tok", [P, CI])
        stat = sb("stat", [P, 2, 6])
        mv = sb("mv", [P, 2])
        rstd = sb("rstd", [P, 2])
        stat2 = sb("stat2", [P, 2, 6])
        mv2 = sb("mv2", [P, 2])
        rstd2 = sb("rstd2", [P, 2])
        nmax = sb("nmax", [P, HEADS])
        rsum = sb("rsum", [P, HEADS])
        rinv = sb("rinv", [P, HEADS])
        norm = sb("norm", [P, 3])
        proj = sb("proj", [P, 3 * DS])
        b_s = sb("b_s", [P, DS])
        proj_t = sb("proj_t", [3 * DS, T])
        dt_t = sb("dt_t", [DS, T])
        a_t = sb("a_t", [DS, T])

        x_raw = sb("x_raw", [P, CI])
        x_r = sb("x_r", [P, 2, CI], f32r)
        b_raw = sb("b_raw", [P, 2, DS])
        b_r = sb("b_r", [P, DS])
        c_blk = sb("c_blk", [P, 2, BT])
        a_blk = sb("a_blk", [P, 2, BT])
        b_bd = sb("b_bd", [P, 2, QT, GB, DS], f32r)
        c_bd = sb("c_bd", [P, BT, 32])
        h_new = sb("h_new", [P, CI])
        h = sb("h", [P, 2, CI])
        y_sb = sb("y_sb", [P, 2, 2, H])

        y_tok = sb("y_tok", [P, CI])
        xn_o = sb("xn_o", [P, CI])
        gate_o = sb("gate_o", [P, CM, T])
        x1_o = sb("x1_o", [P, HM, T])

        ones = x_raw[:, 0:P]
        cond_t = y_sb[:].rearrange("p f q c -> p (f q c)")[:, 0:2 * HM * NB].rearrange("p (k b) -> p k b", b=NB)

        pu = [ctx.enter_context(nc.psum_tensor(f"pu{i}", [P, CI], f32)) for i in range(2)]
        py = ctx.enter_context(nc.psum_tensor("py", [P, 512], f32))
        pa = ctx.enter_context(nc.psum_tensor("pa", [P, 512], f32))
        pi = ctx.enter_context(nc.psum_tensor("pi", [P, 512], f32))
        po = ctx.enter_context(nc.psum_tensor("po", [P, 512], f32))

        def chunks(ap, n=4):
            return ap.rearrange("p (m t) -> p m t", m=n)

        s_in = sem("inputs_loaded")
        s_zero = sem("constants_set")
        s_sq = sem("squares_ready")
        s_dc = sem("dcoef_sums_in_psum")
        s_dcv = sem("dcoef_sums_kept")
        s_sqrt = sem("sqrt_ready")
        s_a0 = sem("tanh_a_log_ready")
        s_wgb = sem("w_x_scaled")
        s_wsum = sem("column_sums_in_psum")
        s_set = sem("setup_step_done")
        s_table = sem("setup_done")
        att_full, att_free = sem("attention_bank_full"), sem("attention_bank_free")
        inn_full, inn_free = sem("inner_bank_full"), sem("inner_bank_free")
        out_full, out_free = sem("out_bank_full"), sem("out_bank_free")
        s_x = sem("x_loaded")
        s_res = sem("residual_loaded")
        s_fac = sem("factors_ready")
        s_xs = sem("x_styled")
        s_st = sem("stats_ready")
        s_mv = sem("mean_var_ready")
        s_ve = sem("var_eps_ready")
        s_rs = sem("rstd_ready")
        s_xn = sem("xn_ready")
        s_mx = sem("neg_max_ready")
        s_ri = sem("reciprocal_sum_ready")
        s_pr = sem("prob_ready")
        s_xres = sem("x1_with_x_ready")
        s_x1 = sem("x1_ready")
        s_c3 = sem("conv_tap3_ready")
        s_cv = sem("conv_step_done")
        s_th = sem("tanh_xc_ready")
        s_sl = sem("silu_ready")
        s_thg = sem("tanh_gate_ready")
        s_st2 = sem("inner_stats_ready")
        s_mv2 = sem("inner_mean_var_ready")
        s_ve2 = sem("inner_var_eps_ready")
        s_rs2 = sem("inner_rstd_ready")
        s_hat = sem("inner_xhat_ready")
        s_xg = sem("inner_xhat_times_g_ready")
        s_xnt = sem("inner_xn_ready")
        s_ss = sem("sum_of_squares_ready")
        s_ssm = sem("bounded_sum_of_squares_ready")
        s_nm = sem("norm_ready")
        s_b = sem("scaled_b_ready")
        s_a = sem("decay_ready")
        s_x1st = sem("x1_stored")
        s_gst = sem("gate_stored")
        s_xst = sem("xn_stored")
        s_bst = sem("b_stored")
        s_cst = sem("c_stored")
        s_ast = sem("decay_stored")
        s_blk = [sem("block_loaded_even"), sem("block_loaded_odd")]
        s_bbd = sem("b_blockdiag_ready")
        s_cbd = sem("c_blockdiag_ready")
        s_u = sem("update_in_psum")
        s_hn = sem("state_summed")
        s_h = sem("state_clipped")
        s_y = sem("y_in_psum")
        s_yk = sem("y_kept")
        s_yst = [sem("y_stored_even_quarters"), sem("y_stored_odd_quarters")]
        s_ol = sem("out_inputs_loaded")
        s_dx = sem("d_times_xn_ready")
        s_yd = sem("y_plus_d_xn_ready")
        s_fin = sem("result_ready")
        s_out = sem("result_stored")
        s_mark = sem("mark_behind_a_wait")
        s_q = [sem("quarter_loaded_even"), sem("quarter_loaded_odd")]
        s_hi = sem("x_hi_ready")
        s_parts = sem("x_parts_ready")
        s_bhi = sem("b_hi_ready")
        s_bp = sem("b_parts_ready")
        BLOCK_DMAS, QUARTER_DMAS = 2, 2 * TERMS

        block = ctx.enter_context(nc.Block())


        def iterations(eng, one):
            for first, end in SPANS:
                if end - first == 1:
                    one(first, first % 2, first)
                else:
                    with eng.Fori(0, (end - first) // 2) as pair:
                        for odd in range(2):
                            one(pair * 2 + (first + odd), (first + odd) % 2, first)

        def attends(first):
            return first < NB

        def has_inner(first):
            return INNER <= first < NB + INNER

        def scans(first):
            return SCAN <= first < NB + SCAN

        def outputs(first):
            return OUT <= first < NB + OUT

        def done_of(use, uses, n):
            return n * len(uses) + uses.index(use) + 1

        def before(use, uses, n):
            return n * len(uses) + uses.index(use)

        def row(dram, n):
            return dram[bass.ds(n, 1)].rearrange("o p c -> (o p) c")

        def grouped(dram, n):
            return dram[bass.ds(n // GB, 1), bass.ds(n % GB, 1)].rearrange("g b t c -> (g b t) c")

        def quartered(dram, n):
            return dram[bass.ds(n // GB, 1), :, bass.ds(n % GB, 1)].rearrange("g q b t c -> (g q b) t c")

        def loads(first, quarter):
            if quarter >= QUARTERS - 2:
                return SCAN - 1 <= first < NB + SCAN - 1
            return scans(first)

        def prefetches(first, quarter):
            if quarter == QUARTERS - 1:
                return SCAN - 1 <= first < NB + SCAN - 1
            return scans(first)

        def flat(ap):
            return ap.rearrange("p m t -> p (m t)")

        @block.sync
        def _(sp):
            for dst, name in ((w5[:], "w5"), (w_in[:], "w_in"), (w_out[:], "w_out"), (w_x[:], "w_x"),
                              (ident[:], "ident"), (mask_b[:], "mask_b"), (mask_c[:], "mask_c"),
                              (cond_t, "cond_t"), (w_dt[2 * DS:3 * DS, :], "w_dt"),
                              (small[0:DS, 0:1], "b_dt"), (small[0:DS, 1:2], "a_log"), (cvec[:], "cvec")):
                sp.dma_start(dst, a[name]).then_inc(s_in, 16)
            for j, name in enumerate(("ln_g_row", "ln_b_row", "d_row")):
                sp.dma_start(rows[:, j, :], a[name].broadcast_to([P, CI])).then_inc(s_in, 16)

            def load_block(n, par):
                for dst, dram in ((c_blk, c_d), (a_blk, a_d)):
                    sp.dma_start(dst[:, par, :], dram[bass.ds(n // GB, 1), :, :, bass.ds((n % GB) * BT, BT)]
                                 .rearrange("g b d t -> (g b d) t")).then_inc(s_blk[par], 16)

            def load_quarter(n, quarter):
                for term in range(TERMS):
                    r = slice(32 * term, 32 * term + 32)
                    for dst, dram in ((x_raw[r, :], xn_d), (b_raw[r, quarter % 2, :], b_d)):
                        src = dram[bass.ds(n // GB, 1), bass.ds((n % GB) * QUARTERS + quarter, 1)]
                        sp.dma_start(dst, src.rearrange("g q b t c -> (g q b t) c")).then_inc(s_q[quarter % 2], 16)

            def store_y(n, quarter):
                sp.wait_ge(s_yk, START + n * 8 + 2 * quarter + 2)
                for odd in range(2):
                    for half in range(2):
                        q0 = 32 * (2 * odd + half)
                        t0 = (n % GB) * BT + 4 * quarter
                        dst = y_d[bass.ds(n // GB, 1), :, bass.ds(t0, 4), half * H:(half + 1) * H]
                        dst = dst.rearrange("g b (e o) c -> (g b) e o c", o=2)[:, :, odd, :]
                        sp.dma_start(dst, y_sb[q0:q0 + GB, quarter % 2, :, :]).then_inc(s_yst[quarter % 2], 16)

            def await_group(i, first):
                ready = (i - INNER) if has_inner(first) else NB
                for stored in (s_xst, s_bst, s_cst, s_ast):
                    sp.wait_ge(stored, START + ready * 16)
                sp.sem_inc(s_mark, 1)

            def one(i, par, first):
                if attends(first):
                    n = i
                    sp.wait_ge(att_free, START + n * len(ATT_USES))
                    sp.dma_start(x_tok, row(a["x"], n)).then_inc(s_x, 16)
                    sp.dma_start(s1_row, a["cond"][bass.ds(n, 1), 0:H].broadcast_to([P, H])).then_inc(s_x, 16)
                if outputs(first):
                    m = i - OUT
                    for stored in s_yst:
                        sp.wait_ge(stored, START + (i - SCAN if scans(first) else NB) * 128)
                        sp.sem_inc(s_mark, 1)
                    sp.wait_ge(s_out, START + m * 16)
                    sp.sem_inc(s_mark, 1)
                    sp.dma_start(y_tok[:], grouped(y_d, m)).then_inc(s_ol, 16)
                    sp.dma_start(xn_o[:], quartered(xn_d, m)).then_inc(s_ol, 16)
                    sp.dma_start(flat(gate_o[:]), row(gate_d, m)).then_inc(s_ol, 16)
                    sp.dma_start(flat(x1_o[:]), row(x1_d, m)).then_inc(s_ol, 16)
                for quarter in range(4):
                    if loads(first, quarter):
                        if quarter == QUARTERS - 2:
                            await_group(i, first)
                        nth = (i - SCAN) * QUARTERS + quarter
                        if first >= SCAN or quarter == QUARTERS - 1:
                            sp.wait_ge(s_parts, nth + 2)
                            sp.sem_inc(s_mark, 1)
                        carry, nxt = divmod(quarter + 2, QUARTERS)
                        load_quarter(i - SCAN + carry, nxt)
                    if scans(first):
                        store_y(i - SCAN, quarter)
                    if quarter == 1 and SCAN - 1 <= first < NB + SCAN - 1:
                        n = i - SCAN + 1
                        await_group(i, first)
                        if first >= SCAN:
                            sp.wait_ge(s_y, Y0 + (i - SCAN) * BT)
                        load_block(n, par ^ 1)
                    if quarter == 1 and has_inner(first):
                        n = i - INNER
                        sp.wait_ge(inn_free, START + done_of("g1", INN_USES, n))
                        sp.dma_start(row(gate_d, n), flat(gate[:])).then_inc(s_gst, 16)
                    if quarter == 2 and attends(first):
                        sp.wait_ge(att_full, done_of("pv", ATT_USES, i))
                        sp.dma_start(flat(x_res), row(a["x_t"], i)).then_inc(s_res, 16)
                if has_inner(first):
                    n = i - INNER
                    sp.wait_ge(s_xnt, n + 1)
                    sp.dma_start(quartered(xn_d, n), xn_tok[:]).then_inc(s_xst, 16)
                    sp.wait_ge(s_b, n + 1)
                    sp.dma_start(quartered(b_d, n), b_s[:]).then_inc(s_bst, 16)
                    sp.wait_ge(inn_free, START + done_of("projT", INN_USES, n))
                    sp.dma_start(grouped(c_d, n), proj_t[DS:2 * DS, :]).then_inc(s_cst, 16)
                    sp.wait_ge(s_a, n + 1)
                    sp.dma_start(grouped(a_d, n), a_t[:]).then_inc(s_ast, 16)
                if attends(first):
                    n = i
                    sp.wait_ge(s_x1, START + n + 1)
                    sp.dma_start(row(x1_d, n), flat(x1_t[:])).then_inc(s_x1st, 16)
                if outputs(first):
                    m = i - OUT
                    sp.wait_ge(s_fin, START + m + 1)
                    sp.dma_start(row(a["out"], m), flat(x1_o[:])).then_inc(s_out, 16)

            sp.wait_ge(s_table, 1)
            iterations(sp, one)
            sp.wait_ge(s_out, START + 16 * NB)

        @block.gpsimd
        def _(pool):
            nc.gpsimd.memset(half_n[:], -0.5).then_inc(s_zero, 1)
            nc.gpsimd.memset(half_p[:], 0.5).then_inc(s_zero, 1)
            pool.wait_ge(s_table, 1)

            def take_apart(n, quarter):
                nth = n * QUARTERS + quarter
                pool.drain()
                pool.wait_ge(s_hi, nth + 1)
                low = x_r[64:128, quarter % 2, :].bitcast(f32)
                nc.gpsimd.tensor_tensor(x_r[64:128, quarter % 2, :], x_raw[64:128, :], low, ALU.subtract).then_inc(s_parts, 1)
                pool.drain()
                pool.wait_ge(s_bhi, nth + 1)
                for r in (slice(32, 64), slice(96, 128)):
                    last = nc.gpsimd.tensor_tensor(b_r[r, :], b_raw[r, quarter % 2, :], b_r[r, :], ALU.subtract)
                last.then_inc(s_bp, 1)
                pool.wait_ge(s_bp, nth + 1)
                nc.gpsimd.tensor_tensor(
                    b_bd[:, quarter % 2], b_r[:, None, None, :].to_broadcast([P, QT, GB, DS]),
                    mask_b[:, :, :, None].to_broadcast([P, QT, GB, DS]), ALU.mult).then_inc(s_bbd, 1)

            def attention(s, n, par):
                if s == 0:
                    pool.wait_ge(s_x, (n + 1) * 32)
                    nc.gpsimd.tensor_tensor(x_tok, x_tok, s1_row, ALU.mult).then_inc(s_xs, 1)
                if s == 2:
                    pool.wait_ge(s_table, 1)
                    pool.wait_ge(s_mv, n + 1)
                    nc.gpsimd.tensor_scalar(rstd[:, 0:1], mv[:, 1:2], EPS_IN, 1.0, ALU.add, ALU.mult).then_inc(s_ve, 1)
                    pool.wait_ge(s_ve, n + 1)
                    nc.gpsimd.tensor_tensor(rstd[:, 1:2], rstd[:, 0:1], half_n[:], ALU.pow).then_inc(s_rs, 1)
                if 7 <= s <= 10:
                    m = s - 7
                    pool.wait_ge(s_ri, n * 4 + m + 1)
                    nc.gpsimd.tensor_tensor(
                        prob[:, m % 2], prob[:, m % 2],
                        rinv[:, 4 * m:4 * m + 4, None].to_broadcast([P, 4, T]), ALU.mult).then_inc(s_pr, 1)
                if s == 13:
                    pool.wait_ge(att_free, START + done_of("w", ATT_USES, n))
                    pool.wait_ge(s_res, (n + 1) * 16)
                    nc.gpsimd.tensor_tensor(x1_t[:], x1_t[:], x_res, ALU.add).then_inc(s_xres, 1)
                if s == 14:
                    pool.wait_ge(att_free, START + done_of("u", ATT_USES, n))
                    pool.wait_ge(s_xres, START + n + 1)
                    nc.gpsimd.tensor_tensor(x1_t[:], x1_t[:], vs_t[:], ALU.add).then_inc(s_x1, 1)

            def inner(s, n, par):
                if s == 9:
                    pool.wait_ge(s_table, 1)
                    pool.wait_ge(s_mv2, n + 1)
                    nc.gpsimd.tensor_scalar(rstd2[:, 0:1], mv2[:, 1:2], 4 * EPS_LN, 1.0, ALU.add, ALU.mult).then_inc(s_ve2, 1)
                    pool.wait_ge(s_ve2, n + 1)
                    nc.gpsimd.tensor_tensor(rstd2[:, 1:2], rstd2[:, 0:1], half_n[:], ALU.pow).then_inc(s_rs2, 1)
                if s == 10:
                    pool.wait_ge(s_hat, n + 1)
                    nc.gpsimd.tensor_tensor(xn_tok[:], xn_tok[:], rows[:, 0, :], ALU.mult).then_inc(s_xg, 1)
                    pool.wait_ge(s_xg, n + 1)
                    nc.gpsimd.tensor_tensor(xn_tok[:], xn_tok[:], rows[:, 1, :], ALU.add).then_inc(s_xnt, 1)
                if s == 13:
                    pool.wait_ge(s_ssm, n + 1)
                    nc.gpsimd.tensor_tensor(norm[:, 2:3], norm[:, 1:2], half_p[:], ALU.pow).then_inc(s_nm, 1)

            def output(s, m, par):
                if s == 2:
                    pool.wait_ge(s_ol, (m + 1) * 64)
                    nc.gpsimd.tensor_tensor(xn_o[:], xn_o[:], rows[:, 2, :], ALU.mult).then_inc(s_dx, 1)
                    pool.wait_ge(s_dx, m + 1)
                    nc.gpsimd.tensor_tensor(y_tok[:], y_tok[:], xn_o[:], ALU.add).then_inc(s_yd, 1)

            def one(i, par, first):
                for s in range(SLOTS):
                    if s % QT == 1 and prefetches(first, s // QT):
                        carry, nxt = divmod(s // QT + 1, QUARTERS)
                        take_apart(i - SCAN + carry, nxt)
                    if attends(first):
                        attention(s, i, par)
                    if has_inner(first):
                        inner(s, i - INNER, par)
                    if outputs(first):
                        output(s, i - OUT, par)

            iterations(pool, one)

        @block.scalar
        def _(act):
            act.wait_ge(s_in, 16 * 15)
            nc.scalar.activation(flat(th[:])[:, 0:2 * HM * NB], cond_t.rearrange("p k b -> p (k b)"), ACT.Square).then_inc(s_sq, 1)
            for w in range(5):
                if w:
                    act.wait_ge(s_dc, w)
                nc.scalar.activation(k_bd[:].rearrange("p m j t -> p (m j t)"),
                                     w5[:, w].rearrange("p k o -> p (k o)"), ACT.Square).then_inc(s_sq, 1)
            act.wait_ge(s_dcv, 5)
            nc.scalar.activation(xn_tok[:, 0:5 * P], xn_tok[:, 0:5 * P], ACT.Sqrt).then_inc(s_sqrt, 1)
            nc.scalar.activation(a_coef[:], small[0:DS, 1:2], ACT.Tanh).then_inc(s_a0, 1)
            act.wait_ge(s_table, 1)

            def high_parts(n, quarter):
                nth = n * QUARTERS + quarter
                act.wait_ge(s_q[quarter % 2], (nth + 2 - quarter % 2) * (8 * QUARTER_DMAS))
                act.wait_ge(s_u, U0 + nth * QT - QT)
                nc.scalar.activation(x_r[:, quarter % 2, :], x_raw[:], ACT.Copy).then_inc(s_hi, 1)
                act.wait_ge(s_bbd, START + nth)
                nc.scalar.activation(b_r[:].bitcast(f32r), b_raw[:, quarter % 2, :], ACT.Copy).then_inc(s_bhi, 1)

            def scan(s, n, par):
                if s % 2 == 1:
                    p = s // 2
                    act.wait_ge(s_y, Y0 + n * BT + s + 1)
                    if p % 2 == 0:
                        act.wait_ge(s_yst[(p // 2) % 2], START + n * 128 + (p // 4) * 64)
                    nc.scalar.activation(y_sb[:, (p // 2) % 2, p % 2, :], py[:], ACT.Copy).then_inc(s_yk, 1)

            def attention(s, n, par):
                def drain(use, dst, src):
                    act.wait_ge(att_full, done_of(use, ATT_USES, n))
                    nc.scalar.activation(dst, src, ACT.Copy).then_inc(att_free, 1)

                def exponentials(m):
                    act.wait_ge(s_mx, n * 4 + m + 1)
                    if m >= 2:
                        act.wait_ge(att_full, done_of(f"p{m - 2}", ATT_USES, n))
                    for j in range(4):
                        hd = 4 * m + j
                        last = nc.scalar.activation(prob[:, m % 2, j, :], chunks(pa[:])[:, j, :], ACT.Exp,
                                                    bias=nmax[:, hd:hd + 1], accum_out=rsum[:, hd:hd + 1])
                    last.then_inc(att_free, 1)

                if s == 3:
                    act.wait_ge(s_x1, START + n)
                    drain("xnT", xn_t[:], chunks(pa[:]))
                if s == 4:
                    act.wait_ge(att_full, done_of("k", ATT_USES, n))
                    for j in range(4):
                        r = slice(32 * j, 32 * j + 32)
                        last = nc.scalar.activation(k_bd[r, :, j, :], chunks(pa[r, :]), ACT.Copy)
                    last.then_inc(att_free, 1)
                if s == 5:
                    drain("v", v_tok[:], pa[:])
                if s in (9, 11):
                    drain(f"p{s - 8}", prob_t[:, s - 8], chunks(pa[:]))
                if 6 <= s <= 9:
                    exponentials(s - 6)

            def inner(s, n, par):
                if s in (0, 1):
                    act.wait_ge(inn_free, START + done_of(f"xr{s}", INN_USES, n))
                    for c in range(4 * s, 4 * s + 4):
                        last = nc.scalar.activation(xc[:, c, :], xr[:, c, 3:3 + T], ACT.Identity,
                                                    bias=cvec[:, c, 4:5], scale=cvec[:, c, 3:4])
                    last.then_inc(s_c3, 1)
                if s in (2, 3):
                    hh = s - 2
                    act.wait_ge(inn_full, done_of(f"g{hh}", INN_USES, n))
                    act.wait_ge(s_sl, START + n * 2)
                    nc.scalar.activation(th[:], chunks(pi[:]), ACT.Tanh, scale=0.5).then_inc(s_thg, 1)
                if s in (4, 5):
                    hh = s - 4
                    act.wait_ge(s_cv, n * 24 + 12 * hh + 12)
                    act.wait_ge(inn_free, START + done_of("g1", INN_USES, n))
                    act.wait_ge(s_sl, START + n * 2 + hh)
                    nc.scalar.activation(th[:], xc[:, 4 * hh:4 * hh + 4], ACT.Tanh, scale=0.5).then_inc(s_th, 1)
                if s in (6, 7):
                    hh = s - 6
                    act.wait_ge(inn_full, done_of(f"c{hh}", INN_USES, n))
                    if hh == 0:
                        act.wait_ge(s_xst, START + n * 16)
                    nc.scalar.activation(xn_tok[:, H * hh:H * hh + H], pi[:], ACT.Copy).then_inc(inn_free, 1)
                if s == 12:
                    act.wait_ge(s_xnt, n + 1)
                    act.wait_ge(inn_full, done_of("proj", INN_USES, n))
                    nc.scalar.activation(flat(xc[:]), xn_tok[:], ACT.Square, accum_out=norm[:, 0:1]).then_inc(s_ss, 1)
                if s == 13:
                    act.wait_ge(inn_full, done_of("projT", INN_USES, n))
                    act.wait_ge(s_cst, START + n * 16)
                    nc.scalar.activation(proj_t[:], pi[0:3 * DS, 0:T], ACT.Copy).then_inc(inn_free, 1)
                if s == 14:
                    act.wait_ge(inn_full, done_of("dt", INN_USES, n))
                    nc.scalar.activation(dt_t[:], pi[0:DS, 0:T], ACT.Tanh, bias=small[0:DS, 0:1]).then_inc(inn_free, 1)

            def one(i, par, first):
                for s in range(SLOTS):
                    if scans(first) and s:
                        scan(s - 1, i - SCAN, par)
                    if s % QT == 1 and prefetches(first, s // QT):
                        carry, nxt = divmod(s // QT + 1, QUARTERS)
                        high_parts(i - SCAN + carry, nxt)
                    if attends(first):
                        attention(s, i, par)
                    if has_inner(first):
                        inner(s, i - INNER, par)
                if scans(first):
                    scan(SLOTS - 1, i - SCAN, par)

            iterations(act, one)

        @block.vector
        def _(dve):
            count = [0]

            def step(ins):
                count[0] += 1
                ins.then_inc(s_set, 1)
                dve.wait_ge(s_set, count[0])

            nc.vector.memset(ones, 1.0).then_inc(s_u, U0)
            nc.vector.memset(xr[:, :, 0:3], 0.0).then_inc(s_hn, SUM0)
            nc.vector.memset(a_t[:, 0:1], 0.0).then_inc(s_y, Y0)
            nc.vector.memset(h[:], 0.0)
            dve.wait_ge(s_in, 16 * 15)
            wg, wb = flat(gate[:])[:, 0:CM * 48], flat(xc[:])[:, 0:CM * 48]
            for dst, col in ((wg, 5), (wb, 6)):
                step(nc.vector.tensor_tensor(chunks(dst, CM), w_x[:], cvec[:, :, col:col + 1].to_broadcast([P, CM, 48]), ALU.mult))
            step(nc.vector.memset(mv[:], 0.0))
            nc.vector.memset(mv2[:], 0.0).then_inc(s_wgb, 1)
            dve.wait_ge(s_wsum, 1)
            step(nc.vector.tensor_scalar(proj[:], pi[:, 0:48], 1.0 / CI, None, ALU.mult))
            step(nc.vector.tensor_tensor(w_x[:], chunks(wg, CM), proj[:, None, :].to_broadcast([P, CM, 48]), ALU.subtract))
            step(nc.vector.tensor_copy(w_x0[:], pi[:, 48:96]))
            for w in range(5):
                dve.wait_ge(s_dc, w + 1)
                nc.vector.tensor_scalar(xn_tok[:, w * P:(w + 1) * P], pa[:, 0:P], EPS_DM, None, ALU.add).then_inc(s_dcv, 1)
            dve.wait_ge(s_sqrt, 1)
            dve.wait_ge(s_dcv, 5)
            step(nc.vector.reciprocal(xn_tok[:, 0:5 * P], xn_tok[:, 0:5 * P]))
            dc = xn_tok[:, 0:5 * P].rearrange("p (w m b) -> p w m b", w=5, m=HM)

            def column(c, n):
                return table[:, :, c:c + n].rearrange("p b m -> p m b")

            step(nc.vector.scalar_tensor_tensor(out=column(QK, HM), in0=dc[:, 0], scalar=DH ** -0.5, in1=dc[:, 1],
                                                op0=ALU.mult, op1=ALU.mult))
            step(nc.vector.tensor_tensor(column(VF, HM), dc[:, 2], cond_t[:, HM:2 * HM, :], ALU.mult))
            step(nc.vector.tensor_copy(column(WF, HM), dc[:, 3]))
            step(nc.vector.tensor_copy(column(UF, HM), dc[:, 4]))
            step(nc.vector.tensor_copy(column(TE, CM), cond_t))
            dve.wait_ge(s_a0, 1)
            step(nc.vector.tensor_scalar(a_coef[:], a_coef[:], -0.01, None, ALU.mult))
            dve.wait_ge(s_zero, 2)
            step(nc.vector.memset(k_bd[:].rearrange("p m j t -> p (m j t)"), 0.0))
            for counts in (att_free, inn_free, out_free, s_xres, s_out, s_xst, s_bst, s_cst, s_ast, s_x1st, s_gst,
                           s_x1, s_bbd, s_h, s_sl, s_yk, s_fin, *s_yst):
                dve.sem_inc(counts, START)
            nc.vector.memset(x1_o[:], 0.0).then_inc(s_table, 1)

            def scan(s, n, par):
                if s == 0:
                    dve.wait_ge(s_blk[par], (n + 2 - par) * (8 * BLOCK_DMAS))
                    dve.wait_ge(s_y, Y0 + n * BT)
                    nc.vector.tensor_tensor(c_bd[:], c_blk[:, par, :, None].to_broadcast([P, BT, 32]),
                                            mask_c[:, None, :].to_broadcast([P, BT, 32]), ALU.mult).then_inc(s_cbd, 1)
                t = n * BT + s
                dve.wait_ge(s_u, U0 + t + 1)
                dve.wait_ge(s_h, START + t)
                nc.vector.scalar_tensor_tensor(out=h_new[:], in0=h[:, (s + 1) % 2, :], scalar=a_blk[:, par, s:s + 1],
                                               in1=pu[s % 2][:], op0=ALU.mult, op1=ALU.add).then_inc(s_hn, 1)
                dve.wait_ge(s_hn, SUM0 + t + 1)
                dve.wait_ge(s_y, Y0 + t - 1)
                nc.vector.tensor_scalar(h[:, s % 2, :], h_new[:], -LIM, LIM, ALU.max, ALU.min).then_inc(s_h, 1)

            def attention(s, n, par):
                def factors(c):
                    return fac[:, par, c:c + HM, None].to_broadcast([P, HM, T])

                def scaled(use, dst, c):
                    dve.wait_ge(att_full, done_of(use, ATT_USES, n))
                    nc.vector.tensor_tensor(dst, chunks(pa[:]), factors(c), ALU.mult).then_inc(att_free, 1)

                if s == 0:
                    nc.vector.tensor_copy(fac[:, par, :], table[:, bass.ds(n, 1), :].rearrange("p o c -> p (o c)")).then_inc(s_fac, 1)
                if s == 2:
                    dve.wait_ge(s_xs, n + 1)
                    nc.vector.bn_stats(stat[:, 0, :], x_tok).then_inc(s_st, 1)
                    dve.wait_ge(s_table, 1)
                    dve.wait_ge(s_st, n + 1)
                    nc.vector.bn_aggr(mv[:], stat[:, 0, :]).then_inc(s_mv, 1)
                if s == 2:
                    dve.wait_ge(s_rs, n + 1)
                    nc.vector.tensor_scalar(x_tok, x_tok, mv[:, 0:1], rstd[:, 1:2], ALU.subtract, ALU.mult).then_inc(s_xn, 1)
                if s == 3:
                    dve.wait_ge(s_fac, n + 1)
                    scaled("q", q_t[:], QK)
                if s == 6:
                    scaled("vT", vs_t[:], VF)
                if 7 <= s <= 10:
                    m = s - 7
                    dve.wait_ge(att_free, START + done_of(f"s{m}", ATT_USES, n))
                    nc.vector.reciprocal(rinv[:, 4 * m:4 * m + 4], rsum[:, 4 * m:4 * m + 4]).then_inc(s_ri, 1)
                if s in (8, 10):
                    m = s - 8
                    dve.wait_ge(att_full, done_of(f"p{m}", ATT_USES, n))
                    nc.vector.tensor_copy(prob_t[:, m], chunks(pa[:])).then_inc(att_free, 1)
                if 6 <= s <= 9:
                    m = s - 6
                    dve.wait_ge(att_full, done_of(f"s{m}", ATT_USES, n))
                    nc.vector.tensor_reduce(nmax[:, 4 * m:4 * m + 4], chunks(pa[:]), AX.X, ALU.max, negate=True).then_inc(s_mx, 1)
                if s == 12:
                    scaled("pv", o_t[:], VF)
                if s == 13:
                    dve.wait_ge(s_x1st, START + n * 16)
                    scaled("w", x1_t[:], WF)
                if s == 14:
                    scaled("u", vs_t[:], UF)

            def inner(s, n, par):
                if s in (0, 1):
                    dve.wait_ge(inn_full, done_of(f"xr{s}", INN_USES, n))
                    te = fac[:, par ^ 1, TE + 4 * s:TE + 4 * s + 4, None].to_broadcast([P, 4, T])
                    nc.vector.tensor_tensor(xr[:, 4 * s:4 * s + 4, 3:], chunks(pi[:]), te, ALU.add).then_inc(inn_free, 1)
                if s in (1, 2):
                    hh = s - 1
                    dve.wait_ge(s_c3, n * 2 + hh + 1)
                    for k in range(3):
                        for c in range(4 * hh, 4 * hh + 4):
                            if k:
                                dve.wait_ge(s_cv, n * 24 + 12 * hh + 4 * (k - 1) + c % 4 + 1)
                            nc.vector.scalar_tensor_tensor(out=xc[:, c, :], in0=xr[:, c, k:k + T], scalar=cvec[:, c, k:k + 1],
                                                           in1=xc[:, c, :], op0=ALU.mult, op1=ALU.add).then_inc(s_cv, 1)
                if s in (2, 3):
                    hh = s - 2
                    dve.wait_ge(s_thg, n * 2 + hh + 1)
                    if hh == 0:
                        dve.wait_ge(s_gst, START + n * 16)
                    nc.vector.scalar_tensor_tensor(out=gate[:, 4 * hh:4 * hh + 4], in0=th[:], scalar=1.0,
                                                   in1=chunks(pi[:]), op0=ALU.add, op1=ALU.mult).then_inc(inn_free, 1)
                if s in (4, 5):
                    hh = s - 4
                    dve.wait_ge(s_th, n * 2 + hh + 1)
                    nc.vector.scalar_tensor_tensor(out=xc[:, 4 * hh:4 * hh + 4], in0=th[:], scalar=1.0,
                                                   in1=xc[:, 4 * hh:4 * hh + 4], op0=ALU.add, op1=ALU.mult).then_inc(s_sl, 1)
                if s in (7, 8):
                    hh = s - 7
                    dve.wait_ge(inn_free, START + done_of(f"c{hh}", INN_USES, n))
                    nc.vector.bn_stats(stat2[:, hh, :], xn_tok[:, H * hh:H * hh + H]).then_inc(s_st2, 1)
                if s == 8:
                    dve.wait_ge(s_table, 1)
                    dve.wait_ge(s_st2, n * 2 + 2)
                    nc.vector.bn_aggr(mv2[:], stat2[:]).then_inc(s_mv2, 1)
                if s == 10:
                    dve.wait_ge(s_rs2, n + 1)
                    nc.vector.tensor_scalar(xn_tok[:], xn_tok[:], mv2[:, 0:1], rstd2[:, 1:2], ALU.subtract, ALU.mult).then_inc(s_hat, 1)
                    dve.wait_ge(inn_full, done_of("proj", INN_USES, n))
                    nc.vector.scalar_tensor_tensor(out=proj[:], in0=pi[:, 0:48], scalar=rstd2[:, 1:2], in1=w_x0[:],
                                                   op0=ALU.mult, op1=ALU.add).then_inc(inn_free, 1)
                if s == 13:
                    dve.wait_ge(s_ss, n + 1)
                    nc.vector.tensor_scalar(norm[:, 1:2], norm[:, 0:1], 1.0, None, ALU.min).then_inc(s_ssm, 1)
                if s == 15:
                    dve.wait_ge(inn_free, START + done_of("dt", INN_USES, n))
                    dve.wait_ge(s_nm, n + 1)
                    dve.wait_ge(s_bst, START + n * 16)
                    nc.vector.tensor_scalar(b_s[:], proj[:, 0:DS], norm[:, 2:3], None, ALU.mult).then_inc(s_b, 1)
                    dve.wait_ge(s_ast, START + n * 16)
                    nc.vector.tensor_scalar(a_t[:, 1:T], dt_t[:, 1:T], a_coef[:], 1.0, ALU.mult, ALU.add).then_inc(s_a, 1)

            def output(s, m, par):
                if s in (4, 6):
                    hh = (s - 4) // 2
                    dve.wait_ge(out_full, done_of(f"yT{hh}", OUT_USES, m))
                    g = gate_o[:, 4 * hh:4 * hh + 4]
                    nc.vector.tensor_tensor(g, g, chunks(po[:]), ALU.mult).then_inc(out_free, 1)
                if s == 14:
                    dve.wait_ge(out_full, done_of("out", OUT_USES, m))
                    nc.vector.scalar_tensor_tensor(out=x1_o[:], in0=chunks(po[:]), scalar=0.5, in1=x1_o[:],
                                                   op0=ALU.mult, op1=ALU.add).then_inc(s_fin, 1)

            def others(s, i, par, first):
                if attends(first):
                    attention(s, i, par)
                if has_inner(first):
                    inner(s, i - INNER, par)
                if outputs(first):
                    output(s, i - OUT, par)

            def one(i, par, first):
                for s in range(SLOTS):
                    if scans(first):
                        scan(s, i - SCAN, par)
                    if s:
                        others(s - 1, i, par, first)
                others(SLOTS - 1, i, par, first)

            iterations(dve, one)

        @block.tensor
        def _(pe):
            pe.wait_ge(s_wgb, 1)
            pe.wait_ge(s_set, 3)
            for j, src in enumerate((flat(gate[:]), flat(xc[:]))):
                for k in range(CM):
                    last = nc.tensor.matmul(pi[:, 48 * j:48 * j + 48], ones, src[:, 48 * k:48 * k + 48],
                                            start=(k == 0), stop=(k == CM - 1))
            last.then_inc(s_wsum, 1)
            squares = k_bd[:].rearrange("p m j t -> p m (j t)")
            for w in range(5):
                pe.wait_ge(s_sq, w + 2)
                if w:
                    pe.wait_ge(s_dcv, w)
                style = HM * (w > 2)
                for m in range(HM):
                    for k in range(HM):
                        last = nc.tensor.matmul(pa[:, NB * m:NB * m + NB], squares[:, k, P * m:P * m + P],
                                                flat(th[:])[:, NB * (style + k):NB * (style + k + 1)],
                                                start=(k == 0), stop=(k == HM - 1))
                last.then_inc(s_dc, 1)
            pe.wait_ge(s_table, 1)

            def product(dst, w, rhs, m):
                for k in range(len(rhs)):
                    last = nc.tensor.matmul(dst, w[:, k, P * m:P * m + P], rhs[k],
                                            start=(k == 0), stop=(k == len(rhs) - 1))
                return last

            def update(s, n, par):
                q = s // QT % 2
                if s % QT == 0:
                    nth = n * QUARTERS + s // QT
                    pe.wait_ge(s_parts, nth + 1)
                    pe.wait_ge(s_bbd, START + nth + 1)
                pe.wait_ge(s_hn, SUM0 + n * BT + s - 1)
                lhs = b_bd[:, q, s % QT].rearrange("p b d -> p (b d)")
                for half in range(2):
                    r = slice(H * half, H * half + H)
                    last = nc.tensor.matmul(pu[s % 2][:, r], lhs, x_r[:, q, r], start=True, stop=True)
                last.then_inc(s_u, 1)

            def read_out(s, n, par):
                if s == 0:
                    pe.wait_ge(s_cbd, n + 1)
                if s % 2 == 0:
                    pe.wait_ge(s_yk, START + n * 8 + s // 2)
                pe.wait_ge(s_h, START + n * BT + s + 1)
                for half in range(2):
                    q0 = 32 * (2 * (s % 2) + half)
                    last = nc.tensor.matmul(py[q0:q0 + 32, :], c_bd[:, s, :], h[:, s % 2, H * half:H * half + H],
                                            start=True, stop=True)
                last.then_inc(s_y, 1)

            def attention(s, n, par):
                def begin(use):
                    pe.wait_ge(att_free, START + before(use, ATT_USES, n))

                def transposes(use, src):
                    begin(use)
                    for j in range(4):
                        last = nc.tensor.transpose(pa[:, P * j:P * j + P], src(j), ident[:])
                    last.then_inc(att_full, 1)

                def layer(use, w, src):
                    begin(use)
                    for m in range(HM):
                        last = product(pa[:, P * m:P * m + P], w5[:, w], [src[:, k, :] for k in range(HM)], m)
                    last.then_inc(att_full, 1)

                def scores(m):
                    begin(f"s{m}")
                    nc.tensor.matmul(pa[:], q_t[:, m, :], k_bd[:, m].rearrange("p j t -> p (j t)"),
                                     start=True, stop=True).then_inc(att_full, 1)

                def turned(m):
                    pe.wait_ge(s_pr, n * 4 + m + 1)
                    transposes(f"p{m}", lambda j: prob[:, m % 2, j, :])

                if s == 3:
                    pe.wait_ge(s_xn, n + 1)
                    transposes("xnT", lambda j: x_tok[:, P * j:P * j + P])
                if s == 3:
                    layer("q", 0, xn_t)
                if s == 4:
                    layer("k", 1, xn_t)
                if s == 5:
                    begin("v")
                    for k in range(HM):
                        last = nc.tensor.matmul(pa[:], xn_t[:, k, :], w5[:, 2, k, :], start=(k == 0), stop=(k == HM - 1))
                    last.then_inc(att_full, 1)
                if s == 6:
                    transposes("vT", lambda j: v_tok[:, P * j:P * j + P])
                    scores(0)
                if s == 7:
                    scores(1)
                if s == 8:
                    turned(0)
                    scores(2)
                if s == 9:
                    turned(1)
                    scores(3)
                if s == 10:
                    turned(2)
                if s == 11:
                    turned(3)
                if s == 12:
                    begin("pv")
                    for m in range(HM):
                        for j in range(4):
                            hd = 4 * m + j
                            last = nc.tensor.matmul(pa[32 * j:32 * j + 32, P * m:P * m + P], v_tok[:, DH * hd:DH * hd + DH],
                                                    prob_t[:, m, j, :], start=True, stop=True)
                    last.then_inc(att_full, 1)
                if s == 13:
                    layer("w", 3, o_t)
                if s == 14:
                    layer("u", 4, vs_t)

            def inner(s, n, par):
                def begin(use):
                    pe.wait_ge(inn_free, START + before(use, INN_USES, n))

                if s < 4:
                    use = ("xr0", "xr1", "g0", "g1")[s]
                    if s == 0:
                        pe.wait_ge(s_x1, START + n + 1)
                    begin(use)
                    for m in range(4):
                        last = product(pi[:, P * m:P * m + P], w_in, [x1_t[:, k, :] for k in range(HM)], 4 * s + m)
                    last.then_inc(inn_full, 1)
                if s in (6, 7):
                    hh = s - 6
                    pe.wait_ge(s_sl, START + n * 2 + hh + 1)
                    begin(f"c{hh}")
                    for j in range(4):
                        last = nc.tensor.transpose(pi[:, P * j:P * j + P], xc[:, 4 * hh + j, :], ident[:])
                    last.then_inc(inn_full, 1)
                if s == 8:
                    begin("proj")
                    for k in range(CM):
                        last = nc.tensor.matmul(pi[:, 0:48], xc[:, k, :], w_x[:, k, :], start=(k == 0), stop=(k == CM - 1))
                    last.then_inc(inn_full, 1)
                if s == 12:
                    begin("projT")
                    pe.sem_inc(s_mark, 1)
                    nc.tensor.transpose(pi[0:48, 0:T], proj[:], ident[:]).then_inc(inn_full, 1)
                if s == 14:
                    begin("dt")
                    pe.sem_inc(s_mark, 1)
                    nc.tensor.matmul(pi[0:DS, 0:T], w_dt[2 * DS:3 * DS, :], proj_t[2 * DS:3 * DS, :],
                                     start=True, stop=True).then_inc(inn_full, 1)

            def output(s, m, par):
                if s in (4, 6):
                    hh = (s - 4) // 2
                    pe.wait_ge(s_yd, m + 1)
                    pe.wait_ge(out_free, START + m * 2 + hh)
                    if hh == 0:
                        pe.wait_ge(s_fin, START + m)
                    for j in range(4):
                        c0 = P * (4 * hh + j)
                        last = nc.tensor.transpose(po[:, P * j:P * j + P], y_tok[:, c0:c0 + P], ident[:])
                    last.then_inc(out_full, 1)
                if 10 <= s <= 13:
                    if s == 10:
                        pe.wait_ge(out_free, START + m * 2 + 2)
                    last = product(po[:, P * (s - 10):P * (s - 9)], w_out, [gate_o[:, k, :] for k in range(CM)], s - 10)
                    if s == 13:
                        last.then_inc(out_full, 1)

            def one(i, par, first):
                for s in range(SLOTS):
                    if scans(first):
                        if s == 0:
                            update(0, i - SCAN, par)
                        if s + 1 < SLOTS:
                            update(s + 1, i - SCAN, par)
                        if s:
                            read_out(s - 1, i - SCAN, par)
                    if attends(first):
                        attention(s, i, par)
                    if has_inner(first):
                        inner(s, i - INNER, par)
                    if outputs(first):
                        output(s, i - OUT, par)
                if scans(first):
                    read_out(SLOTS - 1, i - SCAN, par)

            iterations(pe, one)


def kernel(x, cond_2048, L0_cond_q_weight, L0_cond_k_weight, L0_cond_v_weight, L0_cond_w_weight, L0_cond_u_weight,
           L1_cond_W_in, L1_cond_W_conv, L1_cond_b_conv, L1_cond_ln_g, L1_cond_ln_b, L1_cond_W_xproj, L1_cond_W_dt,
           L1_cond_b_dt, L1_cond_A_log, L1_cond_D, L1_cond_W_out):
    import concourse.bacc as bacc
    from concourse.bass_utils import run_bass_kernel_spmd

    def turned(w):
        w = np.asarray(w)
        o, i = w.shape
        return w.T.reshape(i // P, P, o).transpose(1, 0, 2)

    def by_channel(v):
        v = np.asarray(v)
        return v.reshape(CM, P, -1).transpose(1, 0, 2)

    x, cond = np.asarray(x), np.asarray(cond_2048)
    row, step = np.arange(P)[:, None], np.arange(QT)[None, :]
    arrays = {
        "x": x,
        "x_t": x.transpose(0, 2, 1).reshape(NB, HM, P, T).transpose(0, 2, 1, 3).reshape(NB, P, HM * T),
        "cond": cond,
        "cond_t": cond.T.reshape(2 * HM, P, NB).transpose(1, 0, 2),
        "w5": np.stack([turned(w) for w in (L0_cond_q_weight, L0_cond_k_weight, L0_cond_v_weight,
                                            L0_cond_w_weight, L0_cond_u_weight)], 1),
        "w_in": turned(L1_cond_W_in),
        "w_out": turned(L1_cond_W_out),
        "w_x": turned(L1_cond_W_xproj),
        "w_dt": np.asarray(L1_cond_W_dt).T,
        "b_dt": np.asarray(L1_cond_b_dt)[:, None],
        "a_log": np.asarray(L1_cond_A_log)[:, None],
        "cvec": np.concatenate([by_channel(np.asarray(L1_cond_W_conv).reshape(CI, 4)), by_channel(L1_cond_b_conv),
                                by_channel(L1_cond_ln_g), by_channel(L1_cond_ln_b)], 2),
        "ln_g_row": np.asarray(L1_cond_ln_g)[None, :],
        "ln_b_row": np.asarray(L1_cond_ln_b)[None, :],
        "d_row": np.asarray(L1_cond_D)[None, :],
        "ident": np.eye(P, dtype=np.float32),
        "mask_b": ((row % QT == step)[:, :, None] & (row // QT % GB == np.arange(GB)[None, :])[:, None, :]).astype(np.float32),
        "mask_c": (row // DS == np.arange(32)[None, :]).astype(np.float32),
    }
    arrays = {k: np.ascontiguousarray(v) for k, v in arrays.items()}
    nc = bacc.Bacc("TRN2", target_bir_lowering=False, num_devices=1)
    aps = {k: nc.dram_tensor(f"in_{k}", v.shape, mybir.dt.from_np(v.dtype), kind="ExternalInput").ap()
           for k, v in arrays.items()}
    aps["out"] = nc.dram_tensor("out_t", (NB, P, HM * T), mybir.dt.float32, kind="ExternalOutput").ap()
    build(nc, aps)
    r = run_bass_kernel_spmd(nc, [{f"in_{k}": v for k, v in arrays.items()}], core_ids=[0])
    out = np.asarray(r.results[0]["out_t"])
    return out.reshape(NB, P, HM, T).transpose(0, 3, 2, 1).reshape(NB, T, H)
```
